# Optimizing a Trainium2 kernel written in Bass

```python
import numpy as np
import jax
import jax.numpy as jnp

def _softmax(x, axis=-1):
    return jax.nn.softmax(x, axis=axis)

def _gelu(x):
    return jax.nn.gelu(x, approximate=True)

def _silu(x):
    return jax.nn.silu(x)

def _sigmoid(x):
    return jax.nn.sigmoid(x)

def _layernorm(x, axis=-1, eps=1e-05):
    m = jnp.mean(x, axis=axis, keepdims=True)
    v = jnp.var(x, axis=axis, keepdims=True)
    return (x - m) / jnp.sqrt(v + eps)

def _scatter_add(tgt, idx, src, axis=0):
    return tgt.at[idx].add(src)

def _segment_sum(src, seg, n):
    return jax.ops.segment_sum(src, seg, n)
kernel_name = 'mk_flamingo_gated_d2_seqx_r8_a09579'

def setup_inputs(seed: int=0):
    np.random.seed(seed)
    _w = jnp.asarray

    def _rec_inputs():
        import jax
        import jax.numpy as jnp
        _rk = jax.random.key(seed)
        x = -0.0002928 + 1 * jax.random.normal(jax.random.fold_in(_rk, 1), (32, 56, 128), jnp.float32)
        _lenS = 56 - jax.random.randint(jax.random.fold_in(_rk, 7), (32,), 0, max(1, 56 // 4) + 1, jnp.int32)
        _lenS2 = 1500 - jax.random.randint(jax.random.fold_in(_rk, 8), (32,), 0, max(1, 1500 // 4) + 1, jnp.int32)
        _ctx_1024P = jax.random.normal(jax.random.fold_in(_rk, 11), (32, 16, 128), jnp.float32)
        _ctx_1024c = jax.random.dirichlet(jax.random.fold_in(_rk, 511), 0.3 * jnp.ones((16,), jnp.float32), (32, 1500))
        _ctx_1024t = jnp.einsum('bsk,bkd->bsd', _ctx_1024c, _ctx_1024P)
        _ctx_1024t = _ctx_1024t * jax.lax.rsqrt(jnp.mean(jnp.square(_ctx_1024t)) + 1e-12) * 0.953939
        ctx_1024 = -1.39393e-06 + 0.999914 * (_ctx_1024t + 0.3 * jax.random.normal(jax.random.fold_in(_rk, 611), (32, 1500, 128), jnp.float32))
        fside_1x16xSxS2_0 = 3.01377e-06 + 0.0200011 * jax.random.normal(jax.random.fold_in(_rk, 12), (1, 16, 56, 1500), jnp.float32)
        _g = jax.random.normal(jax.random.fold_in(_rk, 9001), (2, 2), jnp.float32)
        _g = jnp.sign(_g) * jnp.maximum(jnp.abs(_g), 1.0) + (_g == 0) * 1.0
        g_xattn = _g[0]
        g_ffn = _g[1]
        return (x, ctx_1024, fside_1x16xSxS2_0, g_xattn, g_ffn)
    x, ctx_1024, fside_1x16xSxS2_0, g_xattn, g_ffn = _rec_inputs()

    def _L0_xattn_setup():
        import jax, jax.numpy as jnp
        import numpy as np
        N_HEADS = 16

        def _split_heads(x, n_heads):
            B, S, D = x.shape
            return x.reshape(B, S, n_heads, D // n_heads).transpose(0, 2, 1, 3)
        key = jax.random.key(seed)
        ks = jax.random.split(key, 5)
        B, S, D = (2, 256, 128)
        H = N_HEADS
        return {'queries': jax.random.normal(ks[0], (B, S, D), dtype=jnp.float32), 'keys': jax.random.normal(ks[1], (B, S, D), dtype=jnp.float32), 'values': jax.random.normal(ks[2], (B, S, D), dtype=jnp.float32), 'bias': jax.random.normal(ks[3], (1, H, S, S), dtype=jnp.float32) * 0.02, 'w_out': jax.random.normal(ks[4], (D, D), dtype=jnp.float32) * (1.0 / np.sqrt(D))}
    _L0_xattn_all = _L0_xattn_setup()
    _L0_xattn_in = {k: v for k, v in _L0_xattn_all.items() if k in ('w_out',)}
    del _L0_xattn_all

    def _L0_ffn_setup():
        import jax, jax.numpy as jnp
        import numpy as np
        D_MODEL = 128
        D_FF = 512
        N_EXPERTS = 8
        TOP_K = 2
        D_FF_PER = D_FF // N_EXPERTS
        B, T = (4, 256)
        key = jax.random.key(seed)
        ks = jax.random.split(key, 7)
        b1_bound = 1.0 / np.sqrt(D_MODEL)
        b2_bound = 1.0 / np.sqrt(D_FF_PER)
        return {'x': jax.random.normal(ks[0], (B, T, D_MODEL), dtype=jnp.float32), 'router_w': jax.random.uniform(ks[1], (D_MODEL, N_EXPERTS), minval=-b1_bound, maxval=b1_bound, dtype=jnp.float32), 'router_b': jax.random.uniform(ks[2], (N_EXPERTS,), minval=-b1_bound, maxval=b1_bound, dtype=jnp.float32), 'W1': jax.random.uniform(ks[3], (N_EXPERTS, D_MODEL, D_FF_PER), minval=-b1_bound, maxval=b1_bound, dtype=jnp.float32), 'b1': jax.random.uniform(ks[4], (N_EXPERTS, D_FF_PER), minval=-b1_bound, maxval=b1_bound, dtype=jnp.float32), 'W2': jax.random.uniform(ks[5], (N_EXPERTS, D_FF_PER, D_MODEL), minval=-b2_bound, maxval=b2_bound, dtype=jnp.float32), 'b2': jax.random.uniform(ks[6], (N_EXPERTS, D_MODEL), minval=-b2_bound, maxval=b2_bound, dtype=jnp.float32)}
    _L0_ffn_all = _L0_ffn_setup()
    _L0_ffn_in = {k: v for k, v in _L0_ffn_all.items() if k in ('router_w', 'router_b', 'W1', 'b1', 'W2', 'b2')}
    del _L0_ffn_all

    def _L1_xattn_setup():
        import jax, jax.numpy as jnp
        import numpy as np
        B, LQ, LKV, D = (32, 32, 512, 128)
        key0 = jax.random.key(seed)
        kq, kk, kv = jax.random.split(key0, 3)
        query = jax.random.normal(kq, (B, LQ, D), dtype=jnp.float32)
        key = jax.random.normal(kk, (B, LKV, D), dtype=jnp.float32)
        value = jax.random.normal(kv, (B, LKV, D), dtype=jnp.float32)
        scale_factor = jnp.float32(1.0 / np.sqrt(D))
        dropout_p = 0
        return {'query': query, 'key': key, 'value': value, 'scale_factor': scale_factor, 'dropout_p': dropout_p}
    _L1_xattn_all = _L1_xattn_setup()
    _L1_xattn_in = {k: v for k, v in _L1_xattn_all.items() if k in ('scale_factor',)}
    del _L1_xattn_all

    def _L1_ffn_setup():
        import jax, jax.numpy as jnp
        import numpy as np
        N_EMBD = 128
        NUM_EXPERTS = 8
        TOP_K = 2
        D_FF = 4 * N_EMBD
        B, S = (4, 256)
        key = jax.random.key(seed)
        ks = jax.random.split(key, 7)
        scale = lambda fan_in: 1.0 / np.sqrt(fan_in)
        x = jax.random.normal(ks[0], (B, S, N_EMBD), dtype=jnp.float32)
        W_router = jax.random.normal(ks[1], (N_EMBD, NUM_EXPERTS), dtype=jnp.float32) * scale(N_EMBD)
        b_router = jnp.zeros((NUM_EXPERTS,), dtype=jnp.float32)
        W1 = jax.random.normal(ks[2], (NUM_EXPERTS, N_EMBD, D_FF), dtype=jnp.float32) * scale(N_EMBD)
        b1 = jnp.zeros((NUM_EXPERTS, D_FF), dtype=jnp.float32)
        W2 = jax.random.normal(ks[3], (NUM_EXPERTS, D_FF, N_EMBD), dtype=jnp.float32) * scale(D_FF)
        b2 = jnpp = jnp.zeros((NUM_EXPERTS, N_EMBD), dtype=jnp.float32)
        return {'x': x, 'W_router': W_router, 'b_router': b_router, 'W1': W1, 'b1': b1, 'W2': W2, 'b2': b2}
    _L1_ffn_all = _L1_ffn_setup()
    _L1_ffn_in = {k: v for k, v in _L1_ffn_all.items() if k in ('W_router', 'b_router', 'W1', 'b1', 'W2', 'b2')}
    del _L1_ffn_all
    return {'x': x, 'ctx_1024': ctx_1024, 'fside_1x16xSxS2_0': fside_1x16xSxS2_0, 'g_xattn': g_xattn, 'g_ffn': g_ffn, 'L0_xattn_w_out': _L0_xattn_in['w_out'], 'L0_ffn_router_w': _L0_ffn_in['router_w'], 'L0_ffn_router_b': _L0_ffn_in['router_b'], 'L0_ffn_W1': _L0_ffn_in['W1'], 'L0_ffn_b1': _L0_ffn_in['b1'], 'L0_ffn_W2': _L0_ffn_in['W2'], 'L0_ffn_b2': _L0_ffn_in['b2'], 'L1_xattn_scale_factor': _L1_xattn_in['scale_factor'], 'L1_ffn_W_router': _L1_ffn_in['W_router'], 'L1_ffn_b_router': _L1_ffn_in['b_router'], 'L1_ffn_W1': _L1_ffn_in['W1'], 'L1_ffn_b1': _L1_ffn_in['b1'], 'L1_ffn_W2': _L1_ffn_in['W2'], 'L1_ffn_b2': _L1_ffn_in['b2']}

def reference(x, ctx_1024, fside_1x16xSxS2_0, g_xattn, g_ffn, L0_xattn_w_out, L0_ffn_router_w, L0_ffn_router_b, L0_ffn_W1, L0_ffn_b1, L0_ffn_W2, L0_ffn_b2, L1_xattn_scale_factor, L1_ffn_W_router, L1_ffn_b_router, L1_ffn_W1, L1_ffn_b1, L1_ffn_W2, L1_ffn_b2):
    import jax
    import jax.numpy as jnp

    def _L0_xattn_ref(queries, keys, values, bias, w_out):
        import jax, jax.numpy as jnp
        import numpy as np
        N_HEADS = 16

        def _split_heads(x, n_heads):
            B, S, D = x.shape
            return x.reshape(B, S, n_heads, D // n_heads).transpose(0, 2, 1, 3)
        H = N_HEADS
        q = _split_heads(queries, H)
        k = _split_heads(keys, H)
        v = _split_heads(values, H)
        hd = k.shape[-1]
        logits = jnp.einsum('bhqd,bhkd->bhqk', q, k) + bias
        weights = jax.nn.softmax(logits * (1.0 / np.sqrt(hd)), axis=-1)
        attn = jnp.einsum('bhqk,bhkd->bhqd', weights, v)
        B, _, Sq, _ = attn.shape
        combined = attn.transpose(0, 2, 1, 3).reshape(B, Sq, H * hd)
        return combined @ w_out

    def _L0_ffn_ref(x, router_w, router_b, W1, b1, W2, b2):
        import jax, jax.numpy as jnp
        import numpy as np
        D_MODEL = 128
        D_FF = 512
        N_EXPERTS = 8
        TOP_K = 2
        D_FF_PER = D_FF // N_EXPERTS
        B, T = (4, 256)
        router_logits = x @ router_w + router_b
        routing_weights = jax.nn.softmax(router_logits, axis=-1)
        top_k_weights, top_k_indices = jax.lax.top_k(routing_weights, TOP_K)
        top_k_weights = top_k_weights / jnp.sum(top_k_weights, axis=-1, keepdims=True)
        routing_mask = jnp.zeros_like(routing_weights)
        routing_mask = jnp.take_along_axis(routing_mask, top_k_indices, axis=-1)
        b_idx = jnp.arange(x.shape[0])[:, None, None]
        t_idx = jnp.arange(x.shape[1])[None, :, None]
        routing_mask = jnp.zeros_like(routing_weights).at[b_idx, t_idx, top_k_indices].set(top_k_weights)
        h1 = jnp.einsum('btd,nde->btne', x, W1) + b1
        h1 = jax.nn.gelu(h1, approximate=False)
        out_per_expert = jnp.einsum('btne,nef->btnf', h1, W2) + b2
        output = jnp.sum(out_per_expert * routing_mask[..., None], axis=-2)
        return output

    def _L1_xattn_ref(query, key, value, scale_factor, dropout_p):
        import jax, jax.numpy as jnp
        import numpy as np
        B, LQ, LKV, D = (32, 32, 512, 128)
        qk = jnp.einsum('bqd,bkd->bqk', query, key)
        softmax_qk = jax.nn.softmax(qk * scale_factor, axis=-1)
        output = jnp.einsum('bqk,bkd->bqd', softmax_qk, value)
        return output

    def _L1_ffn_ref(x, W_router, b_router, W1, b1, W2, b2):
        import jax, jax.numpy as jnp
        import numpy as np
        N_EMBD = 128
        NUM_EXPERTS = 8
        TOP_K = 2
        D_FF = 4 * N_EMBD
        B, S = (4, 256)
        Bv, Sv, D = x.shape
        flat_x = x.reshape(-1, D)
        T = flat_x.shape[0]
        logits = flat_x @ W_router + b_router
        top_vals, top_idx = jax.lax.top_k(logits, TOP_K)
        neg_inf = jnp.full_like(logits, -jnp.inf)
        sparse_logits = neg_inf.at[jnp.arange(T)[:, None], top_idx].set(top_vals)
        router_weights = jax.nn.softmax(sparse_logits, axis=-1)
        final_output = jnp.zeros_like(flat_x)
        for e in range(NUM_EXPERTS):
            expert_mask = jnp.any(top_idx == e, axis=-1)
            h = jax.nn.relu(flat_x @ W1[e] + b1[e])
            y = h @ W2[e] + b2[e]
            w = router_weights[:, e] * expert_mask.astype(x.dtype)
            final_output = final_output + y * w[:, None]
        return final_output.reshape(Bv, Sv, D)
    x = x + jnp.tanh(g_xattn[0]) * _L0_xattn_ref(_layernorm(x, axis=-1), ctx_1024, ctx_1024, fside_1x16xSxS2_0, L0_xattn_w_out)
    x = x + jnp.tanh(g_ffn[0]) * _L0_ffn_ref(_layernorm(x, axis=-1), L0_ffn_router_w, L0_ffn_router_b, L0_ffn_W1, L0_ffn_b1, L0_ffn_W2, L0_ffn_b2)
    x = x + jnp.tanh(g_xattn[1]) * _L1_xattn_ref(_layernorm(x, axis=-1), ctx_1024, ctx_1024, L1_xattn_scale_factor, 0)
    x = x + jnp.tanh(g_ffn[1]) * _L1_ffn_ref(_layernorm(x, axis=-1), L1_ffn_W_router, L1_ffn_b_router, L1_ffn_W1, L1_ffn_b1, L1_ffn_W2, L1_ffn_b2)
    return x

_drawn_inputs = setup_inputs


def setup_inputs(seed=0):
    import zlib

    import numpy as np

    out = dict(_drawn_inputs(seed))
    spreads = {'g_ffn': (-1.0, 0.567),
     'L1_ffn_b_router': (0.0, 0.1),
     'L1_ffn_b1': (0.0, 0.1),
     'L1_ffn_b2': (0.0, 0.1)}
    factors = {'fside_1x16xSxS2_0': 33.876}
    for name, (base, spread) in spreads.items():
        noise = np.random.default_rng([zlib.crc32(name.encode()), seed]).standard_normal(out[name].shape)
        drawn = base * np.exp(spread * noise) if base else spread * noise
        out[name] = jnp.asarray(drawn.astype(out[name].dtype))
    for name, factor in factors.items():
        out[name] = (out[name] * factor).astype(out[name].dtype)
    return out
```

```python
from contextlib import ExitStack

import concourse.bass as bass
from concourse import mybir

ACT = mybir.ActivationFunctionType
ALU = mybir.AluOpType
AX = mybir.AxisListType
F32 = mybir.dt.float32
F16 = mybir.dt.float16

P = 128
B, S, D, S2 = 32, 56, 128, 1500
H = 16
HD = D // H
T = B * S
ROWS = H * S
TILES = ROWS // P
KP = 125
KC = S2 // KP
TH = 3
KT = S2 // TH
CT = KC // TH
KE = KP + 1
KTE = CT * KE
GH = 4
NG = H // GH
GR = GH * S
GD = GH * HD
TERMS = 3
STACKED = 16 * TERMS * NG
ST = TERMS * GD
TT = T // P
NQ = 4
TQ = T // NQ
E = 8
F0, F1 = 64, 512
EPS = 1e-5
BANK = 512
HALF = 64
SCALE0 = HD ** -0.5
ROUTE_EXP = 13
ROUTE_STEPS = 18


def pieces(t):
    out, r = [], t * P
    while r < (t + 1) * P:
        g = r // GR
        n = min((g + 1) * GR, (t + 1) * P) - r
        at = r - t * P
        if n < P:
            n = 64 if n >= 64 and at % 64 == 0 else 32
        out.append((g, r, n))
        r += n
    return out


def flamingo(nc, x, ctx_, bias, g_xattn, g_ffn, w_out, r_w0, r_b0, w1_0, b1_0, w2_0, b2_0, scale1,
             r_w1, r_b1, w1_1, b1_1, w2_1, b2_1, ident, ident16, diag4, diag4h, row_q, row_head,
             sel0, sel1, mean_w, rank, out):
    with ExitStack() as stack:
        def sb(name, shape, dt=F32):
            return stack.enter_context(nc.sbuf_tensor(name, shape, dt))

        def sem(name):
            return stack.enter_context(nc.semaphore(name))

        resid = sb("resid", [P, T])
        normed = sb("normed", [P, T])
        bias_sb = sb("bias_sb", [P, TILES, S2])
        ptT = sb("ptT", [P, KC * ROWS])
        sc = sb("sc", [P, 2, S2])
        kv = sb("kv", [P, 2, KC * D])
        kraw = normed[:, 0:KC * D]
        k16 = sb("k16", [P, 2, KC * D], F16)
        kT16 = sb("kT16", [P, 2, KC * KE], F16)
        kst = sb("kst", [P, 2, NG * KC * KE], F16)
        qst = sb("qst", [P, NG, T], F16)
        qbd = sb("qbd", [P, 2, ROWS], F16)
        h16 = k16[:, :, :].rearrange("p a n -> p (a n)")[:, 0:T]
        l16 = kT16[:, :, :].rearrange("p a n -> p (a n)")[:, 0:T]
        mx = sb("mx", [P, 2, TH])
        negmax = sb("negmax", [P, 2])
        rowsum = sb("rowsum", [P, 2, TILES])
        rs16 = sb("rs16", [P, 2, TILES], F16)
        rsel = sb("rsel", [P, 2, TILES, S], F16)
        o_mask = sb("o_mask", [P, GH, S])
        o_sum = sb("o_sum", [P, S])
        r_inv = sb("r_inv", [P, S])
        comb = sb("comb", [P, S])
        wout_sb = sb("wout_sb", [P, D])
        id_sb = sb("id_sb", [P, P])
        id16_sb = sb("id16_sb", [P, P], F16)
        diag4_sb = sb("diag4_sb", [P, GH])
        diag4h_sb = sb("diag4h_sb", [P, GH], F16)
        rowq_sb = sb("rowq_sb", [P, TILES, S], F16)
        rowhead_sb = sb("rowhead_sb", [P, TILES, P], F16)
        sel0_sb = sb("sel0_sb", [E, E // 2, P])
        sel1_sb = sb("sel1_sb", [E, E, P])
        mean_sb = sb("mean_sb", [P, P])
        rank_sb = sb("rank_sb", [P, E])
        gates_in = sb("gates_in", [P, 4])
        gates = sb("gates", [P, 4])
        scale_sb = sb("scale_sb", [P, 1])
        eps_sb = sb("eps_sb", [P, 1])
        rw_sb = sb("rw_sb", [P, 2, E])
        rb_sb = sb("rb_sb", [P, 2, E])
        w10_sb = sb("w10_sb", [P, E, F0])
        w20_sb = sb("w20_sb", [P, E // 2, D])
        B1R = E // 2 + E * F1 // P
        b1_rows = sb("b1_rows", [B1R, P])
        b1T = sb("b1T", [P, B1R])
        b10_sb = b1T[:, 0:E // 2]
        b11_sb = b1T[:, E // 2:B1R].rearrange("p (e k) -> p e k", e=E)
        b2_sb = sb("b2_sb", [E, 2, D])
        bias_flat = bias_sb[:, :, :].rearrange("p a n -> p (a n)")
        w11_sb = bias_flat[:, 0:E * F1].rearrange("p (e f) -> p e f", e=E)
        w21_sb = bias_flat[:, E * F1:2 * E * F1].rearrange("p (e k d) -> p e k d", e=E, k=F1 // P)
        rt = [sb(f"rt{i}", [P, TT, E]) for i in range(4)]
        rm = sb("rm", [P, 4, TT])
        wT = sb("wT", [E, T])
        sq = ptT[:, 0:T]
        rstd = ptT[:, T:2 * T]
        mix = ptT[:, 2 * T:2 * T + 12 * TQ].rearrange("p (s n) -> p s n", n=TQ)
        k2T = ptT[:, 0:4 * S2].rearrange("p (r u n) -> p r u n", r=2, u=2)
        p2T = ptT[:, 4 * S2:4 * S2 + KC * P].rearrange("p (c n) -> p c n", n=P)
        kst_f = kst[:, :, :].rearrange("p a n -> p (a n)").bitcast(F32)
        kv2 = [[kv[:, 0, :], kv[:, 1, :]], [kst_f[:, 0:KC * D], kst_f[:, KC * D:2 * KC * D]]]
        q2 = sb("q2", [P, 2, 2, HALF])
        o2 = sb("o2", [P, D])
        r2 = sb("r2", [P, 1])
        xin = sc[:, :, :].rearrange("p a n -> p (a n)")[:, 0:T].rearrange("p (i d) -> p i d", d=D)

        ps_s = stack.enter_context(nc.psum_tensor("ps_s", [P, TH, BANK], F32))
        ps_t = stack.enter_context(nc.psum_tensor("ps_t", [P, TH, BANK], F32))
        ps_o = stack.enter_context(nc.psum_tensor("ps_o", [P, BANK], F32))
        ps_m = stack.enter_context(nc.psum_tensor("ps_m", [P, BANK], F32))
        ps_kt = ps_m[:, :].bitcast(F16).rearrange("p (a n) -> p a n", a=2)
        pv_acc = ps_o[:, 0:GR]
        r_acc = ps_o[:, 256:256 + S]

        passed = sem("passed")
        early_in = sem("early_in")
        consts_in = sem("consts_in")
        x_in = sem("x_in")
        bias_in = sem("bias_in")
        xT_raw = sem("xT_raw")
        xT_done = sem("xT_done")
        b1_raw = sem("b1_raw")
        b1_done = sem("b1_done")
        eps_set = sem("eps_set")
        gates_done = sem("gates_done")
        ln_mean = sem("ln_mean")
        ln_cent = sem("ln_cent")
        ln_sq = sem("ln_sq")
        ln_var = sem("ln_var")
        ln_std = sem("ln_std")
        ln_inv = sem("ln_inv")
        ln_done = sem("ln_done")
        q_high = sem("q_high")
        q_low = sem("q_low")
        qst_in = sem("qst_in")
        kraw_in = [sem(f"kraw_in{j}") for j in range(TH)]
        k0_in = [sem(f"k0_in{j}") for j in range(TH)]
        v_in = sem("v_in")
        k_zero = sem("k_zero")
        k_high = sem("k_high")
        k_low = sem("k_low")
        kt_raw = sem("kt_raw")
        kt_done = sem("kt_done")
        kst_in = sem("kst_in")
        q_ready = sem("q_ready")
        scored = sem("scored")
        biased = sem("biased")
        negmaxed = sem("negmaxed")
        probs = sem("probs")
        t_raw = sem("t_raw")
        t_act = sem("t_act")
        t_dve = sem("t_dve")
        rs_part = sem("rs_part")
        rsel_done = sem("rsel_done")
        values_used = sem("values_used")
        attended = sem("attended")
        comb_step = sem("comb_step")
        combined = sem("combined")
        projected = sem("projected")
        updated = sem("updated")
        logits = sem("logits")
        route_step = sem("route_step")
        route_exp = sem("route_exp")
        routed = sem("routed")
        wT_raw = sem("wT_raw")
        wT_done = sem("wT_done")
        hidden0 = sem("hidden0")
        spread0 = sem("spread0")
        gelu_done = sem("gelu_done")
        weighted = sem("weighted")
        y_part = sem("y_part")
        mixed0 = sem("mixed0")
        w1_in = sem("w1_in")
        hidden1 = sem("hidden1")
        hid_act = sem("hid_act")
        hid_dve = sem("hid_dve")
        spread1 = sem("spread1")
        spread_out = sem("spread_out")
        b2_sum = sem("b2_sum")
        acc_set = sem("acc_set")
        y_done = sem("y_done")
        y_mul = sem("y_mul")
        y_add = sem("y_add")
        mixed1 = sem("mixed1")
        ctx2_in = [[sem(f"ctx2_in{r}{u}") for u in range(2)] for r in range(2)]
        q2_zero = sem("q2_zero")
        q2_done = sem("q2_done")
        t2_raw = sem("t2_raw")
        e2_act = sem("e2_act")
        e2_dve = sem("e2_dve")
        scored2 = sem("scored2")
        negmax2 = sem("negmax2")
        probs2 = sem("probs2")
        pv2 = sem("pv2")
        inv2 = sem("inv2")
        normal2 = sem("normal2")
        o2_raw = sem("o2_raw")
        updated2 = sem("updated2")
        out_raw = sem("out_raw")
        out_sb = sem("out_sb")
        stored = sem("stored")

        early = [(id_sb[:, :], ident), (mean_sb[:, :], mean_w)]
        consts = [
            (id16_sb[:, :], ident16), (diag4_sb[:, :], diag4), (diag4h_sb[0:ST, :], diag4h), (rowq_sb[:, :, :], row_q),
            (rowhead_sb[:, :, :], row_head), (wout_sb[:, :], w_out),
            (gates_in[:, 0:2], g_xattn.partition_broadcast(P)), (gates_in[:, 2:4], g_ffn.partition_broadcast(P)),
            (scale_sb[:, :], scale1.partition_broadcast(P)),
            (sel0_sb[:, :, :], sel0), (sel1_sb[:, :, :], sel1), (rank_sb[:, :], rank),
            (rw_sb[:, 0, :], r_w0), (rw_sb[:, 1, :], r_w1),
            (rb_sb[:, 0, :], r_b0.partition_broadcast(P)), (rb_sb[:, 1, :], r_b1.partition_broadcast(P)),
            (w10_sb[:, :, :], w1_0.rearrange("e d f -> d e f")),
            (w20_sb[:, :, :], w2_0.rearrange("(i e) f d -> (e f) i d", e=2)),
            (b1_rows[0:E // 2, :], b1_0.rearrange("(i e) f -> i (e f)", e=2)),
            (b1_rows[E // 2:B1R, :], b1_1.rearrange("e (k p) -> (e k) p", p=P)),
            (b2_sb[:, 0, :], b2_0), (b2_sb[:, 1, :], b2_1),
        ]
        CONSTS = 16 * len(consts)
        ctx_v = ctx_.rearrange("b (c p) d -> b p c d", p=KP)
        bias_v = bias.rearrange("a h q k -> (a h q) k").rearrange("(t p) k -> p t k", p=P)

        def third(j):
            return slice(CT * D * j, CT * D * (j + 1))

        def raw_keys(b, j):
            src = kv[:, 0, :] if isinstance(b, int) and b == 0 else kraw
            return src[0:KP, third(j)]

        NORM_IN = [(xT_done, NQ), (updated, B), (mixed0, NQ), (updated2, B // 2)]

        def chunk(c):
            return slice(TQ * c, TQ * (c + 1))

        def var_bank(c):
            return (ps_o if c % 2 else ps_m)[:, 0:TQ]

        def norm_tensor(pe, r):
            sem_in, n_in = NORM_IN[r]
            pe.wait_ge(sem_in, n_in)

            def mean(c):
                if c >= 2:
                    pe.wait_ge(ln_cent, NQ * r + c - 1)
                pe.matmul(ps_t[:, c % 2, 0:TQ], mean_sb[:, :], resid[:, chunk(c)], start=True, stop=True).then_inc(ln_mean, 1)

            def variance(c):
                pe.wait_ge(ln_sq, NQ * r + c + 1)
                if c >= 2:
                    pe.wait_ge(ln_std, NQ * r + c - 1)
                pe.matmul(var_bank(c), mean_sb[:, :], sq[:, chunk(c)], start=True, stop=True).then_inc(ln_var, 1)

            mean(0)
            for c in range(NQ):
                if c + 1 < NQ:
                    mean(c + 1)
                variance(c)

        def norm_scalar(act, r):
            for c in range(NQ):
                act.wait_ge(ln_cent, NQ * r + c + 1)
                act.activation(sq[:, chunk(c)], normed[:, chunk(c)], ACT.Square).then_inc(ln_sq, 1)
            act.wait_ge(eps_set, 1)
            for c in range(NQ):
                act.wait_ge(ln_var, NQ * r + c + 1)
                act.activation(rstd[:, chunk(c)], var_bank(c), ACT.Sqrt, bias=eps_sb[:, 0:1]).then_inc(ln_std, 1)

        def norm_vector(dve, r):
            for c in range(NQ):
                dve.wait_ge(ln_mean, NQ * r + c + 1)
                dve.tensor_tensor(normed[:, chunk(c)], resid[:, chunk(c)], ps_t[:, c % 2, 0:TQ], ALU.subtract).then_inc(ln_cent, 1)
            for c in range(NQ):
                dve.wait_ge(ln_std, NQ * r + c + 1)
                dve.reciprocal(rstd[:, chunk(c)], rstd[:, chunk(c)]).then_inc(ln_inv, 1)
                dve.wait_ge(ln_inv, NQ * r + c + 1)
                dve.tensor_tensor(normed[:, chunk(c)], normed[:, chunk(c)], rstd[:, chunk(c)], ALU.mult).then_inc(ln_done, 1)

        def four_tiles(i):
            bank = ps_s[:, i // 4, :] if i < 4 * TH else ps_t[:, 0, :]
            return bank[:, P * (i % 4):P * (i % 4 + 1)]

        def route_tensor(pe, layer):
            pe.wait_ge(ln_done, NQ * (2 * layer + 2))
            for i in range(TT):
                last = pe.matmul(ps_o[:, E * i:E * (i + 1)], normed[:, P * i:P * (i + 1)], rw_sb[:, layer, :], start=True, stop=True)
            last.then_inc(logits, 1)
            pe.wait_ge(routed, layer + 1)
            for i in range(TT):
                last = pe.transpose(four_tiles(i)[0:E, :], rt[2][:, i, :], id_sb[:, :])
            last.then_inc(wT_raw, 1)

        def route_scalar(act, layer):
            act.wait_ge(route_step, ROUTE_STEPS * layer + ROUTE_EXP)
            act.activation(rm[:, 3, :], rm[:, 2, :], ACT.Exp).then_inc(route_exp, 1)

        def route_vector(dve, layer):
            step = [ROUTE_STEPS * layer]

            def link(instruction):
                step[0] += 1
                instruction.then_inc(route_step, 1)
                dve.wait_ge(route_step, step[0])

            def per_token(v):
                return v.unsqueeze(2).broadcast_to([P, TT, E])

            def one_hot(dst, src, top):
                link(dve.tensor_reduce(rm[:, top, :], src[:, :, :], axis=AX.X, op=ALU.max))
                link(dve.tensor_tensor(dst[:, :, :], src[:, :, :], per_token(rm[:, top, :]), ALU.is_equal))
                link(dve.tensor_tensor(dst[:, :, :], dst[:, :, :], rank_sb[:, :].unsqueeze(1).broadcast_to([P, TT, E]), ALU.mult))
                link(dve.tensor_reduce(rm[:, 1, :], dst[:, :, :], axis=AX.X, op=ALU.max))
                link(dve.tensor_tensor(dst[:, :, :], dst[:, :, :], per_token(rm[:, 1, :]), ALU.is_equal))

            dve.wait_ge(logits, layer + 1)
            link(dve.tensor_tensor(rt[0][:, :, :], ps_o[:, 0:TT * E].rearrange("p (i e) -> p i e", e=E),
                                   rb_sb[:, layer, :].unsqueeze(1).broadcast_to([P, TT, E]), ALU.add))
            one_hot(rt[1], rt[0], 0)
            link(dve.scalar_tensor_tensor(out=rt[2][:, :, :], in0=rt[1][:, :, :], scalar=-3.0e38, in1=rt[0][:, :, :],
                                          op0=ALU.mult, op1=ALU.add))
            one_hot(rt[3], rt[2], 2)
            link(dve.tensor_tensor(rm[:, 2, :], rm[:, 2, :], rm[:, 0, :], ALU.subtract))
            assert step[0] == ROUTE_STEPS * layer + ROUTE_EXP
            dve.wait_ge(route_exp, layer + 1)
            link(dve.tensor_scalar(rm[:, 0, :], rm[:, 3, :], 1.0, None, ALU.add))
            link(dve.reciprocal(rm[:, 1, :], rm[:, 0, :]))
            link(dve.tensor_tensor(rm[:, 2, :], rm[:, 3, :], rm[:, 1, :], ALU.mult))
            link(dve.tensor_tensor(rt[1][:, :, :], rt[1][:, :, :], per_token(rm[:, 1, :]), ALU.mult))
            link(dve.tensor_tensor(rt[3][:, :, :], rt[3][:, :, :], per_token(rm[:, 2, :]), ALU.mult))
            assert step[0] == ROUTE_STEPS * (layer + 1)
            dve.tensor_tensor(rt[2][:, :, :], rt[1][:, :, :], rt[3][:, :, :], ALU.add).then_inc(routed, 1)
            dve.wait_ge(wT_raw, layer + 1)
            for c in range(NQ):
                n = min(4 * P, T - 4 * P * c)
                bank = ps_s[:, c, :] if c < TH else ps_t[:, 0, :]
                dve.tensor_copy(wT[:, 4 * P * c:4 * P * c + n], bank[0:E, 0:n]).then_inc(wT_done, 1)

        PAIRS = E // 2

        def y0_bank(c):
            return (ps_o if c % 2 else ps_m)[:, 0:TQ]

        def mixture0_tensor(pe):
            route_tensor(pe, 0)
            pe.wait_ge(wT_done, NQ)

            def output(k):
                c, i = divmod(k, PAIRS)
                if i == 0:
                    if c >= 2:
                        pe.wait_ge(mixed0, c - 1)
                    pe.matmul(y0_bank(c), b2_sb[:, 0, :], wT[:, chunk(c)], start=True, stop=False)
                pe.wait_ge(weighted, k + 1)
                pe.matmul(y0_bank(c), w20_sb[:, i, :], mix[:, 2 + k % 2, :], start=False, stop=i == PAIRS - 1).then_inc(y_part, 1)

            for k in range(NQ * PAIRS):
                c, i = divmod(k, PAIRS)
                if k >= 2:
                    pe.wait_ge(gelu_done, k - 1)
                pe.matmul(ps_s[:, k % 2, 0:TQ], w10_sb[:, 2 * i:2 * i + 2, :].rearrange("p e f -> p (e f)"),
                          normed[:, chunk(c)], start=True, stop=True).then_inc(hidden0, 1)
                if k >= 2:
                    pe.wait_ge(weighted, k - 1)
                pe.matmul(ps_t[:, k % 2, 0:TQ], sel0_sb[:, i, :], wT[:, chunk(c)], start=True, stop=True).then_inc(spread0, 1)
                if k >= 1:
                    output(k - 1)
            output(NQ * PAIRS - 1)

        def mixture0_scalar(act):
            route_scalar(act, 0)
            for k in range(NQ * PAIRS):
                act.wait_ge(hidden0, k + 1)
                if k >= 2:
                    act.wait_ge(weighted, k - 1)
                act.activation(mix[:, k % 2, :], ps_s[:, k % 2, 0:TQ], ACT.Gelu, bias=b10_sb[:, k % PAIRS:k % PAIRS + 1]).then_inc(gelu_done, 1)

        def mixture0_vector(dve):
            route_vector(dve, 0)
            for k in range(NQ * PAIRS):
                c, i = divmod(k, PAIRS)
                dve.wait_ge(gelu_done, k + 1)
                dve.wait_ge(spread0, k + 1)
                if k >= 2:
                    dve.wait_ge(y_part, k - 1)
                dve.tensor_tensor(mix[:, 2 + k % 2, :], mix[:, k % 2, :], ps_t[:, k % 2, 0:TQ], ALU.mult).then_inc(weighted, 1)
                if i == PAIRS - 1:
                    dve.wait_ge(y_part, k + 1)
                    dve.scalar_tensor_tensor(out=resid[:, chunk(c)], in0=y0_bank(c), scalar=gates[:, 2:3], in1=resid[:, chunk(c)],
                                             op0=ALU.mult, op1=ALU.add).then_inc(mixed0, 1)

        NP2 = B // 2

        def pairs(eng, pair):
            pair(0, 0, 0)
            with eng.Fori(0, (NP2 - 2) // 2) as i:
                pair(2 * i + 1, 1, i)
                pair(2 * i + 2, 0, i + 1)
            pair(NP2 - 1, 1, NP2 // 2 - 1, last=True)

        def act_before(p):
            return 6 * p + 4

        def dve_before(p):
            return 3 * p + 2

        def turned_before(p):
            return 0 if isinstance(p, int) and p == 0 else 9 * p - 3

        def second_attention_sync(sp):
            def load(p, r):
                for u in range(2):
                    sp.dma_start(kv2[r][u][0:KP, :].rearrange("p (c d) -> p c d", d=D),
                                 ctx_v[bass.ds(2 * p + u, 1), :, :, :].rearrange("a p c d -> p (a c) d")).then_inc(ctx2_in[r][u], 16)

            sp.wait_ge(attended, B)
            load(0, 0)
            for dst, src in ((w11_sb, w1_1.rearrange("e d f -> d e f")),
                             (w21_sb, w2_1.rearrange("e (k p) d -> p e k d", p=P))):
                sp.dma_start(dst, src).then_inc(w1_in, 16)

            def pair(p, r, k, last=False):
                if not last:
                    if not isinstance(p, int) or p > 0:
                        sp.wait_ge(pv2, p)
                        sp.sem_inc(passed, 1)
                    load(p + 1, 1 - r)

            pairs(sp, pair)
            for c in range(NQ):
                n = min(4, TT - 4 * c)
                sp.wait_ge(out_sb, c + 1)
                sp.dma_start(out.rearrange("b s d -> (b s) d")[4 * P * c:4 * P * c + P * n, :].rearrange("(i p) d -> p i d", p=P),
                             xin[:, 4 * c:4 * c + n, :]).then_inc(stored, 16)
            sp.wait_ge(stored, 16 * NQ)

        def second_attention_pool(pool):
            pool.wait_ge(ln_done, NQ * 3)
            pool.memset(q2[:, :, :, :], 0.0).then_inc(q2_zero, 1)
            pool.wait_ge(q2_zero, 1)

            def queries(p, r):
                pool.tensor_tensor(q2[:, r, :, 0:S], normed[:, bass.ds(2 * S * p, 2 * S)].rearrange("p (u q) -> p u q", u=2),
                                   scale_sb[:, 0:1].unsqueeze(2).broadcast_to([P, 2, S]), ALU.mult).then_inc(q2_done, 1)

            queries(0, 0)

            def pair(p, r, k, last=False):
                if not last:
                    if not isinstance(p, int) or p > 0:
                        pool.wait_ge(scored2, p)
                    queries(p + 1, 1 - r)

            pairs(pool, pair)

        def second_attention_scalar(act):
            def keys_out(p, r):
                for u in range(2):
                    for j in range(2):
                        act.wait_ge(t2_raw, turned_before(p) + TH * u + j + 1)
                        act.activation(k2T[:, r, u, KT * j:KT * (j + 1)], ps_t[:, j, 0:KT], ACT.Copy).then_inc(e2_act, 1)

            act.wait_ge(ln_done, NQ * 3)
            keys_out(0, 0)

            def pair(p, r, k, last=False):
                act.wait_ge(negmax2, p + 1)
                act.activation(sc[:, r, :].rearrange("p (j n) -> p j n", j=TH), ps_s[:, :, 0:KT], ACT.Exp, bias=negmax[:, 0:1],
                               accum_out=rowsum[:, 0, 0:1]).then_inc(probs2, 1)
                if not last:
                    keys_out(p + 1, 1 - r)
                for q in range(2):
                    act.wait_ge(t2_raw, 9 * p + (6 if last else 12) + q + 1)
                    act.activation(p2T[0:KP, CT * q:CT * (q + 1), :], ps_t[0:KP, q, :].rearrange("p (c n) -> p c n", n=P),
                                   ACT.Copy).then_inc(e2_act, 1)

            pairs(act, pair)

        def second_attention_vector(dve):
            def keys_out(p, r):
                for u in range(2):
                    dve.wait_ge(t2_raw, turned_before(p) + TH * u + TH)
                    dve.tensor_copy(k2T[:, r, u, 2 * KT:3 * KT], ps_t[:, 2, 0:KT]).then_inc(e2_dve, 1)

            def update(p):
                dve.wait_ge(o2_raw, p + 1)
                r = resid[:, bass.ds(2 * S * p, 2 * S)].rearrange("p (u q) -> p u q", u=2)
                dve.scalar_tensor_tensor(out=r, in0=ps_m[:, 0:P].rearrange("p (u q) -> p u q", u=2)[:, :, 0:S],
                                         scalar=gates[:, 1:2], in1=r, op0=ALU.mult, op1=ALU.add).then_inc(updated2, 1)

            keys_out(0, 0)

            def pair(p, r, k, last=False):
                dve.wait_ge(scored2, p + 1)
                dve.tensor_reduce(negmax[:, 0:1], ps_s[:, :, 0:KT], axis=AX.XY, op=ALU.max, negate=True).then_inc(negmax2, 1)
                if not isinstance(p, int) or p > 0:
                    update(p - 1)
                if not last:
                    keys_out(p + 1, 1 - r)
                dve.wait_ge(t2_raw, 9 * p + (9 if last else 15))
                dve.tensor_copy(p2T[0:KP, 2 * CT:3 * CT, :], ps_t[0:KP, 2, :].rearrange("p (c n) -> p c n", n=P)).then_inc(e2_dve, 1)
                dve.wait_ge(probs2, p + 1)
                dve.reciprocal(r2[:, 0:1], rowsum[:, 0, 0:1]).then_inc(inv2, 1)
                dve.wait_ge(inv2, p + 1)
                dve.wait_ge(pv2, p + 1)
                if not isinstance(p, int) or p > 0:
                    dve.wait_ge(o2_raw, p)
                dve.tensor_scalar(o2[:, :], ps_o[:, 0:D], r2[:, 0:1], None, ALU.mult).then_inc(normal2, 1)

            pairs(dve, pair)
            update(NP2 - 1)

        def second_attention_tensor(pe):
            def keys(p, r, k):
                for u in range(2):
                    pe.wait_ge(ctx2_in[r][u], 16 * (k + 1))
                    for j in range(TH):
                        if not isinstance(p, int) or p > 0:
                            if j < 2:
                                pe.wait_ge(e2_act, act_before(p - 1) - 2 + 2 * u + j + 1)
                            else:
                                pe.wait_ge(e2_dve, dve_before(p - 1) + u)
                        elif u == 1:
                            if j < 2:
                                pe.wait_ge(e2_act, j + 1)
                            else:
                                pe.wait_ge(e2_dve, 1)
                        for c in range(CT):
                            cc = CT * j + c
                            last = pe.transpose(ps_t[:, j, KP * c:KP * (c + 1)], kv2[r][u][0:KP, D * cc:D * (cc + 1)], id_sb[0:KP, 0:KP])
                        last.then_inc(t2_raw, 1)

            def turn_output(p):
                pe.wait_ge(normal2, p + 1)
                pe.transpose(ps_m[:, 0:P], o2[:, :], id_sb[:, :]).then_inc(o2_raw, 1)

            keys(0, 0, 0)

            def pair(p, r, k, last=False):
                pe.wait_ge(q2_done, p + 1)
                pe.wait_ge(e2_act, act_before(p) - (2 if not isinstance(p, int) or p > 0 else 0))
                pe.wait_ge(e2_dve, dve_before(p))
                if not isinstance(p, int) or p > 0:
                    pe.wait_ge(probs2, p)
                for j in range(TH):
                    for u in range(2):
                        last_mm = pe.matmul(ps_s[HALF * u:HALF * (u + 1), j, 0:KT], q2[:, r, u, :], k2T[:, r, u, KT * j:KT * (j + 1)],
                                            start=True, stop=True)
                last_mm.then_inc(scored2, 1)
                if not isinstance(p, int) or p > 0:
                    turn_output(p - 1)
                if not last:
                    keys(p + 1, 1 - r, k + r)
                pe.wait_ge(probs2, p + 1)
                for q in range(TH):
                    if q < 2:
                        pe.wait_ge(e2_act, act_before(p) + (-2 if last else 2) + q + 1)
                    else:
                        pe.wait_ge(e2_dve, dve_before(p) + (0 if last else 2))
                    for c in range(CT):
                        cc = CT * q + c
                        last_mm = pe.transpose(ps_t[0:KP, q, P * c:P * (c + 1)], sc[:, r, KP * cc:KP * (cc + 1)], id_sb[:, :])
                    last_mm.then_inc(t2_raw, 1)
                pe.wait_ge(e2_act, act_before(p) + (2 if last else 6))
                pe.wait_ge(e2_dve, dve_before(p) + (1 if last else 3))
                if not isinstance(p, int) or p > 0:
                    pe.wait_ge(normal2, p)
                for c in range(KC):
                    for u in range(2):
                        last_mm = pe.matmul(ps_o[HALF * u:HALF * (u + 1), 0:D], p2T[0:KP, c, HALF * u:HALF * (u + 1)],
                                            kv2[r][u][0:KP, D * c:D * (c + 1)], start=c == 0, stop=c == KC - 1)
                last_mm.then_inc(pv2, 1)

            pairs(pe, pair)
            turn_output(NP2 - 1)

        FK = F1 // P

        def chunks(eng, body):
            body(0, first=True)
            with eng.Fori(1, NQ) as c:
                body(c)

        def tokens(c):
            return bass.ds(TQ * c, TQ)

        def hidden_bank(f):
            return (ps_s[:, f, 0:TQ] if f < TH else ps_t[:, 0, 0:TQ])

        def y1_bank(e):
            return (ps_o if e % 2 else ps_m)[:, 0:TQ]

        def mixture1_tensor(pe):
            route_tensor(pe, 1)
            pe.wait_ge(wT_done, 2 * NQ)
            pe.wait_ge(w1_in, 32)

            def output(k, e, f):
                if f == 0 and (not isinstance(k, int) or k >= 2):
                    pe.wait_ge(y_mul, k - 1)
                pe.wait_ge(hid_dve if f % 2 else hid_act, FK // 2 * k + f // 2 + 1)
                last = pe.matmul(y1_bank(e), w21_sb[:, e, f, :], mix[:, FK * (e % 2) + f, :], start=f == 0, stop=f == FK - 1)
                if f == FK - 1:
                    last.then_inc(y_done, 1)

            def body(c, first=False):
                for e in range(E):
                    k = E * c + e
                    start = first and e == 0
                    for f in range(FK):
                        if not start:
                            pe.wait_ge(hid_dve if f % 2 else hid_act, FK // 2 * (k - 1) + f // 2 + 1)
                        pe.matmul(hidden_bank(f), w11_sb[:, e, P * f:P * (f + 1)], normed[:, tokens(c)], start=True, stop=True).then_inc(hidden1, 1)
                        if not start:
                            output(k - 1, (e - 1) % E, f)
                    if not start:
                        pe.wait_ge(spread_out, k)
                        pe.sem_inc(passed, 1)
                    pe.matmul(ps_t[:, 1, 0:TQ], sel1_sb[:, e, :], wT[:, tokens(c)], start=True, stop=True).then_inc(spread1, 1)
                    if e == 0:
                        if not first:
                            pe.wait_ge(acc_set, c)
                            pe.sem_inc(passed, 1)
                        pe.matmul(ps_t[:, 2, 0:TQ], b2_sb[:, 1, :], wT[:, tokens(c)], start=True, stop=True).then_inc(b2_sum, 1)

            chunks(pe, body)
            for f in range(FK):
                output(E * NQ - 1, E - 1, f)
            pe.wait_ge(mixed1, NQ)
            for i in range(TT):
                last = pe.transpose(four_tiles(i), resid[:, P * i:P * (i + 1)], id_sb[:, :])
                if i % 4 == 3 or i == TT - 1:
                    last.then_inc(out_raw, 1)

        def mixture1_scalar(act):
            route_scalar(act, 1)

            def body(c, first=False):
                for e in range(E):
                    k = E * c + e
                    for f in range(0, FK, 2):
                        act.wait_ge(hidden1, FK * k + f + 1)
                        if not isinstance(k, int) or k >= 2:
                            act.wait_ge(y_done, k - 1)
                        act.activation(mix[:, FK * (e % 2) + f, :], hidden_bank(f), ACT.Relu, bias=b11_sb[:, e, f:f + 1]).then_inc(hid_act, 1)
                    act.wait_ge(spread1, k + 1)
                    if not isinstance(k, int) or k >= 2:
                        act.wait_ge(y_mul, k - 1)
                    act.activation(mix[:, 2 * FK + e % 2, :], ps_t[:, 1, 0:TQ], ACT.Copy).then_inc(spread_out, 1)

            chunks(act, body)

        def mixture1_vector(dve):
            route_vector(dve, 1)
            prod, total = mix[:, 2 * FK + 2, :], mix[:, 2 * FK + 3, :]

            def weigh(k, e):
                dve.wait_ge(y_done, k + 1)
                dve.wait_ge(spread_out, k + 1)
                if not isinstance(k, int) or k >= 1:
                    dve.wait_ge(y_add, k)
                dve.tensor_tensor(prod, y1_bank(e), mix[:, 2 * FK + e % 2, :], ALU.mult).then_inc(y_mul, 1)
                dve.wait_ge(y_mul, k + 1)
                dve.tensor_tensor(total, total, prod, ALU.add).then_inc(y_add, 1)

            def finish(c):
                dve.wait_ge(y_add, E * (c + 1))
                r = resid[:, tokens(c)]
                dve.scalar_tensor_tensor(out=r, in0=total, scalar=gates[:, 3:4], in1=r, op0=ALU.mult, op1=ALU.add).then_inc(mixed1, 1)

            def body(c, first=False):
                for e in range(E):
                    k = E * c + e
                    for f in range(1, FK, 2):
                        dve.wait_ge(hidden1, FK * k + f + 1)
                        if not isinstance(k, int) or k >= 2:
                            dve.wait_ge(y_done, k - 1)
                        dve.tensor_scalar(mix[:, FK * (e % 2) + f, :], hidden_bank(f), b11_sb[:, e, f:f + 1], 0.0,
                                          ALU.add, ALU.max).then_inc(hid_dve, 1)
                    if not (first and e == 0):
                        weigh(k - 1, (e - 1) % E)
                    if e == 0:
                        if not first:
                            finish(c - 1)
                            dve.wait_ge(mixed1, c)
                        dve.wait_ge(b2_sum, c + 1)
                        dve.tensor_copy(total, ps_t[:, 2, 0:TQ]).then_inc(acc_set, 1)
                        dve.wait_ge(acc_set, c + 1)

            chunks(dve, body)
            weigh(E * NQ - 1, E - 1)
            finish(NQ - 1)
            for c in range(NQ):
                n = min(4, TT - 4 * c)
                dve.wait_ge(out_raw, c + 1)
                bank = ps_s[:, c, :] if c < TH else ps_t[:, 0, :]
                dve.tensor_copy(xin[:, 4 * c:4 * c + n, :].rearrange("p i d -> p (i d)"), bank[:, 0:P * n]).then_inc(out_sb, 1)

        block = stack.enter_context(nc.Block())

        def batches(eng, batch):
            batch(0, 0, first=True)
            with eng.Fori(0, (B - 2) // 2) as i:
                batch(2 * i + 1, 1)
                batch(2 * i + 2, 0)
            batch(B - 1, 1, last=True)

        @block.sync
        def _(sp):
            def load_keys(b, j):
                ready = k0_in[j] if isinstance(b, int) and b == 0 else kraw_in[j]
                sp.dma_start(raw_keys(b, j).rearrange("p (c d) -> p c d", d=D),
                             ctx_v[bass.ds(b, 1), :, CT * j:CT * (j + 1), :].rearrange("a p c d -> p (a c) d")
                             ).then_inc(ready, 16)

            def copy_values(b, u):
                for j in range(TH):
                    sp.wait_ge(kraw_in[j], 16 * b)
                    if not isinstance(b, int):
                        sp.sem_inc(passed, 1)
                sp.dma_start(kv[0:KP, u, :], kraw[0:KP, :]).then_inc(v_in, 16)

            def stack_keys(b, u):
                sp.wait_ge(kt_done, TH * (b + 1))
                if not isinstance(b, int) or b > 1:
                    if not isinstance(b, int):
                        sp.sem_inc(passed, 1)
                    sp.wait_ge(scored, TH * TILES * (b - 1))
                for term, half in enumerate((0, 0, 1)):
                    for g in range(NG):
                        sp.dma_start(kst[GD * term:GD * (term + 1), u, KTE * TH * g:KTE * TH * (g + 1)],
                                     kT16[GD * g:GD * (g + 1), half, :]).then_inc(kst_in, 16)

            for dst, src in early:
                sp.dma_start(dst, src).then_inc(early_in, 16)
            sp.dma_start(xin, x.rearrange("b s d -> (b s) d").rearrange("(i p) d -> p i d", p=P)).then_inc(x_in, 16)
            for j in range(TH):
                load_keys(0, j)
            for dst, src in consts:
                sp.dma_start(dst, src).then_inc(consts_in, 16)
            sp.dma_start(bias_sb[:, :, :], bias_v).then_inc(bias_in, 16)
            for term, (half, ready) in enumerate(((h16, q_high), (l16, q_low), (h16, q_high))):
                sp.wait_ge(ready, 1)
                for g in range(NG):
                    sp.dma_start(qst[GD * term:GD * (term + 1), g, :], half[GD * g:GD * (g + 1), :]).then_inc(qst_in, 16)
            for j in range(TH):
                load_keys(1, j)
            stack_keys(0, 0)

            def batch(b, u):
                if not isinstance(b, int) or b > 0:
                    sp.wait_ge(values_used, b)
                    if not isinstance(b, int):
                        sp.sem_inc(passed, 1)
                copy_values(b + 1, 1 - u)
                if not isinstance(b, int) or b < B - 2:
                    sp.wait_ge(v_in, 16 * (b + 1))
                    if not isinstance(b, int):
                        sp.sem_inc(passed, 1)
                    sp.wait_ge(k_low, TH * (b + 2))
                    if not isinstance(b, int):
                        sp.sem_inc(passed, 1)
                    for j in range(TH):
                        load_keys(b + 2, j)
                stack_keys(b + 1, 1 - u)

            batch(0, 0)
            with sp.Fori(0, (B - 4) // 2) as i:
                batch(2 * i + 1, 1)
                batch(2 * i + 2, 0)
            batch(B - 3, 1)
            batch(B - 2, 0)
            second_attention_sync(sp)

        @block.gpsimd
        def _(pool):
            pool.wait_ge(consts_in, CONSTS)
            pool.wait_ge(ln_done, NQ)
            pool.wait_ge(q_high, 1)
            pool.tensor_tensor(l16, normed[:, :], h16, ALU.subtract).then_inc(q_low, 1)

            def low(b, u, j, first=False):
                pool.wait_ge(k_high, TH * b + j + 1)
                s = third(j)
                pool.tensor_tensor(k16[0:KP, 1, s], raw_keys(b, j), k16[0:KP, 0, s], ALU.subtract).then_inc(k_low, 1)

            def queries(b, u, first=False):
                if not first:
                    pool.wait_ge(scored, TH * TILES * (b - 1))
                for g in range(NG):
                    dst = qbd[0:ST, u, GR * g:GR * (g + 1)].rearrange("p (h q) -> p h q", h=GH)
                    q = qst[0:ST, g, bass.ds(S * b, S)].unsqueeze(1).broadcast_to([ST, GH, S])
                    m = diag4h_sb[0:ST, :].unsqueeze(2).broadcast_to([ST, GH, S])
                    done = pool.tensor_tensor(dst, q, m, ALU.mult)
                done.then_inc(q_ready, 1)

            def row_sums(b, u, first=False):
                pool.wait_ge(probs, TILES * (b + 1))
                if not first:
                    pool.wait_ge(attended, b)
                pool.sem_inc(passed, 1)
                pool.tensor_copy(rs16[:, 0, :], rowsum[:, u, :]).then_inc(rs_part, 1)
                pool.wait_ge(rs_part, 2 * b + 1)
                pool.tensor_tensor(rs16[:, 1, :], rowsum[:, u, :], rs16[:, 0, :], ALU.subtract).then_inc(rs_part, 1)
                pool.wait_ge(rs_part, 2 * b + 2)
                for half in range(2):
                    r = rs16[:, half, :].unsqueeze(2).broadcast_to([P, TILES, S])
                    done = pool.tensor_tensor(rsel[:, half, :, :], rowq_sb[:, :, :], r, ALU.mult)
                done.then_inc(rsel_done, 1)

            for j in range(TH):
                low(0, 0, j, first=True)
            pool.wait_ge(qst_in, STACKED)
            queries(0, 0, first=True)

            def batch(b, u, first=False, last=False):
                if not last:
                    for j in range(TH):
                        low(b + 1, 1 - u, j)
                    queries(b + 1, 1 - u, first=first)
                row_sums(b, u, first=first)

            batches(pool, batch)
            second_attention_pool(pool)

        @block.scalar
        def _(act):
            act.wait_ge(consts_in, CONSTS)
            act.activation(gates[:, :], gates_in[:, :], ACT.Tanh).then_inc(gates_done, 1)
            norm_scalar(act, 0)
            act.wait_ge(ln_done, NQ)
            act.activation(h16, normed[:, :], ACT.Copy).then_inc(q_high, 1)

            def evacuate(b, n, t):
                for q in range(2):
                    act.wait_ge(t_raw, TH * n + q + 1)
                    dst = ptT[0:KP, :].rearrange("p (c r) -> p c r", r=ROWS)
                    act.activation(dst[:, CT * q:CT * (q + 1), P * t:P * (t + 1)],
                                   ps_t[0:KP, q, :].rearrange("p (c r) -> p c r", r=P), ACT.Copy).then_inc(t_act, 1)

            def exponent(n, s, t, u):
                act.wait_ge(negmaxed, n + 1)
                act.activation(sc[:, s, :], sc[:, s, :], ACT.Exp, bias=negmax[:, s:s + 1],
                               accum_out=rowsum[:, u, t:t + 1]).then_inc(probs, 1)

            def batch(b, u, first=False, last=False):
                for t in range(TILES):
                    n = TILES * b + t
                    if not (first and t == 0):
                        evacuate(b, n - 1, (t - 1) % TILES)
                    if t == TILES - 1 and not (first or last):
                        act.wait_ge(rsel_done, b)
                    exponent(n, (u + t) % 2, t, u)

            batches(act, batch)
            evacuate(B - 1, TILES * B - 1, TILES - 1)
            norm_scalar(act, 1)
            mixture0_scalar(act)
            norm_scalar(act, 2)
            second_attention_scalar(act)
            norm_scalar(act, 3)
            mixture1_scalar(act)

        @block.vector
        def _(dve):
            dve.memset(eps_sb[:, :], EPS).then_inc(eps_set, 1)
            for c in range(NQ):
                n = min(4, TT - 4 * c)
                dve.wait_ge(xT_raw, c + 1)
                src = (ps_s[:, c, :] if c < TH else ps_t[:, 0, :])[:, 0:P * n]
                dve.tensor_copy(resid[:, 4 * P * c:4 * P * c + P * n], src).then_inc(xT_done, 1)
            dve.wait_ge(b1_raw, 1)
            dve.tensor_copy(b1T[:, :], ps_o[:, 0:B1R]).then_inc(b1_done, 1)
            norm_vector(dve, 0)

            def high(b, u, j):
                if isinstance(b, int) and b == 0:
                    dve.wait_ge(k0_in[j], 16)
                else:
                    dve.wait_ge(kraw_in[j], 16 * b)
                if not isinstance(b, int) or b > 0:
                    dve.wait_ge(kt_raw, TH * (b - 1) + j + 1)
                dve.tensor_copy(k16[0:KP, 0, third(j)], raw_keys(b, j)).then_inc(k_high, 1)

            def keys_out(b, j):
                dve.wait_ge(kt_raw, TH * b + j + 1)
                if not isinstance(b, int) or b > 0:
                    dve.wait_ge(kst_in, STACKED * b)
                dve.tensor_copy(kT16[:, :, KTE * j:KTE * (j + 1)], ps_kt[:, :, 0:KTE]).then_inc(kt_done, 1)

            def bias_max(n, s, t):
                for j in range(TH):
                    dve.wait_ge(scored, TH * n + j + 1)
                    if j == 0 and (not isinstance(n, int) or n >= 2):
                        dve.wait_ge(t_raw, TH * (n - 1))
                    dve.sem_inc(passed, 1)
                    dve.tensor_tensor_reduce(
                        out=sc[:, s, KT * j:KT * (j + 1)], in0=ps_s[:, j, 0:KT], in1=bias_sb[:, t, KT * j:KT * (j + 1)],
                        scale=SCALE0, scalar=-3.0e38, op0=ALU.add, op1=ALU.max,
                        accum_out=mx[:, s, j:j + 1]).then_inc(biased, 1)
                dve.wait_ge(biased, TH * (n + 1))
                dve.tensor_reduce(negmax[:, s:s + 1], mx[:, s, :], axis=AX.X, op=ALU.max,
                                  negate=True).then_inc(negmaxed, 1)

            def evacuate(n, t):
                dve.wait_ge(t_raw, TH * (n + 1))
                dst = ptT[0:KP, :].rearrange("p (c r) -> p c r", r=ROWS)
                dve.tensor_copy(dst[:, 2 * CT:3 * CT, P * t:P * (t + 1)],
                                ps_t[0:KP, 2, :].rearrange("p (c r) -> p c r", r=P)).then_inc(t_dve, 1)

            def combine(b):
                dve.wait_ge(attended, b + 1)
                m = diag4_sb[:, :].unsqueeze(2).broadcast_to([P, GH, S])
                dve.tensor_tensor(o_mask[:, :, :], pv_acc.rearrange("p (h q) -> p h q", h=GH), m, ALU.mult).then_inc(comb_step, 1)
                dve.reciprocal(r_inv[:, :], r_acc).then_inc(comb_step, 1)
                dve.wait_ge(comb_step, 3 * b + 1)
                dve.tensor_reduce(o_sum[:, :], o_mask[:, :, :].rearrange("p h q -> p q h"), axis=AX.X, op=ALU.add
                                  ).then_inc(comb_step, 1)
                dve.wait_ge(comb_step, 3 * b + 3)
                dve.tensor_tensor(comb[:, :], o_sum[:, :], r_inv[:, :], ALU.mult).then_inc(combined, 1)

            def update(b):
                dve.wait_ge(projected, b + 1)
                r = resid[:, bass.ds(S * b, S)]
                dve.scalar_tensor_tensor(out=r, in0=ps_m[:, 0:S], scalar=gates[:, 0:1], in1=r,
                                         op0=ALU.mult, op1=ALU.add).then_inc(updated, 1)

            dve.wait_ge(qst_in, STACKED)
            dve.memset(k16[96:P, :, :], 0.0).then_inc(k_zero, 1)
            dve.wait_ge(k_zero, 1)
            for j in range(TH):
                high(0, 0, j)
            for j in range(TH):
                keys_out(0, j)
            dve.wait_ge(bias_in, 16)
            dve.wait_ge(gates_done, 1)

            def batch(b, u, first=False, last=False):
                for t in range(TILES):
                    n = TILES * b + t
                    bias_max(n, (u + t) % 2, t)
                    if not (first and t == 0):
                        evacuate(n - 1, (t - 1) % TILES)
                    if not first and t == 1:
                        combine(b - 1)
                    if not first and t == 5:
                        update(b - 1)
                    if not last and t == 0:
                        for j in range(TH):
                            high(b + 1, 1 - u, j)
                    if not last and 1 <= t <= 3:
                        keys_out(b + 1, t - 1)

            batches(dve, batch)
            evacuate(TILES * B - 1, TILES - 1)
            combine(B - 1)
            update(B - 1)
            norm_vector(dve, 1)
            mixture0_vector(dve)
            norm_vector(dve, 2)
            second_attention_vector(dve)
            norm_vector(dve, 3)
            mixture1_vector(dve)

        @block.tensor
        def _(pe):
            pe.wait_ge(early_in, 32)
            pe.wait_ge(x_in, 16)
            for i in range(TT):
                c = i // 4
                dst = (ps_s[:, c, :] if c < TH else ps_t[:, 0, :])[:, P * (i % 4):P * (i % 4 + 1)]
                last = pe.transpose(dst, xin[:, i, :], id_sb[:, :])
                if i % 4 == 3 or i == TT - 1:
                    last.then_inc(xT_raw, 1)
            pe.wait_ge(consts_in, CONSTS)
            pe.transpose(ps_o[:, 0:B1R], b1_rows[:, :], id_sb[0:B1R, 0:B1R]).then_inc(b1_raw, 1)
            pe.wait_ge(b1_done, 1)
            norm_tensor(pe, 0)

            def keys(b, j):
                pe.wait_ge(k_low, TH * b + j + 1)
                if isinstance(b, int) and b == 0:
                    if j > 0:
                        pe.wait_ge(kt_done, j)
                else:
                    pe.wait_ge(kt_done, TH * b + j)
                for half in range(2):
                    for c in range(CT):
                        cc = CT * j + c
                        last = pe.transpose(ps_kt[:, half, KE * c:KE * (c + 1)],
                                            k16[0:KE, half, D * cc:D * (cc + 1)], id16_sb[0:KE, 0:KE])
                last.then_inc(kt_raw, 1)

            def scores(b, u, n, t):
                for j in range(TH):
                    if t == 0:
                        if j == 0:
                            pe.wait_ge(q_ready, b + 1)
                            pe.wait_ge(kst_in, STACKED * (b + 1))
                    if not isinstance(n, int) or n > 0:
                        pe.wait_ge(biased, TH * (n - 1) + j + 1)
                    for g, r, m in pieces(t):
                        at = r - P * t
                        stack_ = kst[0:ST, u, KTE * (TH * g + j):KTE * (TH * g + j + 1)].rearrange("p (c k) -> p c k", k=KE)
                        last = pe.matmul(ps_s[at:at + m, j, 0:KT], qbd[0:ST, u, r:r + m], stack_[:, :, 0:KP],
                                         start=True, stop=True)
                    last.then_inc(scored, 1)

            def transposes(n, s):
                pe.wait_ge(probs, n + 1)
                for q in range(TH):
                    if not isinstance(n, int) or n > 0:
                        if q < 2:
                            pe.wait_ge(t_act, 2 * (n - 1) + q + 1)
                        else:
                            pe.wait_ge(t_dve, n)
                    for c in range(CT):
                        cc = CT * q + c
                        last = pe.transpose(ps_t[0:KP, q, P * c:P * (c + 1)], sc[:, s, KP * cc:KP * (cc + 1)], id_sb[:, :])
                    last.then_inc(t_raw, 1)

            def attend(b, u):
                pe.wait_ge(t_act, 2 * TILES * (b + 1))
                pe.wait_ge(t_dve, TILES * (b + 1))
                pe.wait_ge(v_in, 16 * (B - 1 if isinstance(b, int) and b == B - 1 else b + 1))
                for c in range(KC):
                    for g in range(NG):
                        last = pe.matmul(ps_o[GD * g:GD * (g + 1), 0:GR], kv[0:KP, u, D * c + GD * g:D * c + GD * (g + 1)],
                                         ptT[0:KP, ROWS * c + GR * g:ROWS * c + GR * (g + 1)],
                                         start=c == 0, stop=c == KC - 1)
                last.then_inc(values_used, 1)
                pe.wait_ge(rsel_done, b + 1)
                for t in range(TILES):
                    for half in range(2):
                        last = pe.matmul(r_acc, rowhead_sb[:, t, :], rsel[:, half, t, :],
                                         start=t == 0 and half == 0, stop=t == TILES - 1 and half == 1)
                last.then_inc(attended, 1)

            def project(b):
                pe.wait_ge(combined, b + 1)
                if not isinstance(b, int) or b < B - 1:
                    pe.wait_ge(kt_done, TH * (b + 3) if not isinstance(b, int) or b < B - 2 else TH * B)
                pe.matmul(ps_m[:, 0:S], wout_sb[:, :], comb[:, :], start=True, stop=True).then_inc(projected, 1)

            for j in range(TH):
                keys(0, j)
            scores(0, 0, 0, 0)

            def batch(b, u, first=False, last=False):
                for t in range(TILES):
                    n = TILES * b + t
                    if t < TILES - 1:
                        scores(b, u, n + 1, t + 1)
                    elif not last:
                        scores(b + 1, 1 - u, n + 1, 0)
                    if t == 0 and not first:
                        attend(b - 1, 1 - u)
                    if not last and 1 <= t <= 3:
                        keys(b + 1, t - 1)
                    if t == 4 and not first:
                        project(b - 1)
                    transposes(n, (u + t) % 2)

            batches(pe, batch)
            attend(B - 1, 1)
            project(B - 1)
            norm_tensor(pe, 1)
            mixture0_tensor(pe)
            norm_tensor(pe, 2)
            second_attention_tensor(pe)
            norm_tensor(pe, 3)
            mixture1_tensor(pe)


_INS = ["x", "ctx_1024", "fside_1x16xSxS2_0", "g_xattn", "g_ffn", "L0_xattn_w_out", "L0_ffn_router_w",
        "L0_ffn_router_b", "L0_ffn_W1", "L0_ffn_b1", "L0_ffn_W2", "L0_ffn_b2", "L1_xattn_scale_factor",
        "L1_ffn_W_router", "L1_ffn_b_router", "L1_ffn_W1", "L1_ffn_b1", "L1_ffn_W2", "L1_ffn_b2"]


def _constants():
    import numpy as np

    row = np.arange(ROWS).reshape(TILES, P).T
    part = np.arange(P)
    one = {
        "ident": np.eye(P, dtype=np.float32),
        "ident16": np.eye(P, dtype=np.float16),
        "diag4": (part[:, None] % GD // HD == np.arange(GH)).astype(np.float32),
        "diag4h": (part[:ST, None] % GD // HD == np.arange(GH)).astype(np.float16),
        "row_q": (row[:, :, None] % S == np.arange(S)).astype(np.float16),
        "row_head": (row[:, :, None] // S == part // HD).astype(np.float16),
        "sel0": (np.arange(E)[:, None, None] == 2 * np.arange(E // 2)[:, None] + part // F0).astype(np.float32),
        "sel1": np.broadcast_to(np.eye(E, dtype=np.float32)[:, :, None], (E, E, P)).copy(),
        "mean_w": np.full((P, P), 1.0 / D, np.float32),
        "rank": np.broadcast_to(np.arange(E, 0, -1, dtype=np.float32), (P, E)).copy(),
    }
    return one


def kernel(**inputs):
    import numpy as _np
    import concourse.bacc as _bacc
    from concourse import mybir as _mybir
    from concourse.bass_utils import run_bass_kernel_spmd as _run

    nc = _bacc.Bacc("TRN2", target_bir_lowering=False, num_devices=1)
    arrays, args = {}, []
    for name in _INS:
        a = _np.ascontiguousarray(inputs[name])
        if a.ndim == 0:
            a = a.reshape(1)
        arrays[f"in_{name}_dram"] = a
        args.append(nc.dram_tensor(f"in_{name}_dram", a.shape, _mybir.dt.from_np(a.dtype), kind="ExternalInput").ap())
    for name, a in _constants().items():
        arrays[f"const_{name}_dram"] = a
        args.append(nc.dram_tensor(f"const_{name}_dram", a.shape, _mybir.dt.from_np(a.dtype), kind="ExternalInput").ap())
    args.append(nc.dram_tensor("out_dram", (B, S, D), _mybir.dt.float32, kind="ExternalOutput").ap())
    flamingo(nc, *args)
    r = _run(nc, [arrays], core_ids=[0])
    return r.results[0]["out_dram"]
```

```python
from contextlib import ExitStack

import concourse.bass as bass
from concourse import mybir

ACT = mybir.ActivationFunctionType
ALU = mybir.AluOpType
AX = mybir.AxisListType
F32 = mybir.dt.float32
F16 = mybir.dt.float16

P = 128
B, S, D, S2 = 32, 56, 128, 1500
H = 16
HD = D // H
T = B * S
ROWS = H * S
TILES = ROWS // P
KP = 125
KC = S2 // KP
TH = 3
KT = S2 // TH
CT = KC // TH
KE = KP + 1
KTE = CT * KE
GH = 4
NG = H // GH
GR = GH * S
GD = GH * HD
TERMS = 3
STACKED = 16 * TERMS * NG
ST = TERMS * GD
TT = T // P
NQ = 4
TQ = T // NQ
E = 8
F0, F1 = 64, 512
EPS = 1e-5
BANK = 512
RING = 4
HALF = 64
SCALE0 = HD ** -0.5
ROUTE_EXP = 13
ROUTE_STEPS = 18


def pieces(t):
    out, r = [], t * P
    while r < (t + 1) * P:
        g = r // GR
        n = min((g + 1) * GR, (t + 1) * P) - r
        at = r - t * P
        if n < P:
            n = 64 if n >= 64 and at % 64 == 0 else 32
        out.append((g, r, n))
        r += n
    return out


def flamingo(nc, x, ctx_, bias, g_xattn, g_ffn, w_out, r_w0, r_b0, w1_0, b1_0, w2_0, b2_0, scale1,
             r_w1, r_b1, w1_1, b1_1, w2_1, b2_1, ident, ident16, diag4, diag4h, row_q, row_head,
             sel0, sel1, mean_w, centre_w, rank, out):
    with ExitStack() as stack:
        def sb(name, shape, dt=F32):
            return stack.enter_context(nc.sbuf_tensor(name, shape, dt))

        def sem(name):
            return stack.enter_context(nc.semaphore(name))

        resid = sb("resid", [P, T])
        normed = sb("normed", [P, T])
        bias_sb = sb("bias_sb", [P, TILES, S2])
        ptT = sb("ptT", [P, KC * ROWS])
        sc = sb("sc", [P, 2, S2])
        kv = sb("kv", [P, 2, KC * D])
        kvx = sb("kvx", [P, KC * D])
        ring = [kv[:, 0, :], kv[:, 1, :], kvx[:, :], normed[:, 0:KC * D]]
        k16 = sb("k16", [P, 2, KC * D], F16)
        kT16 = sb("kT16", [P, 2, KC * KE], F16)
        kst = sb("kst", [P, 2, NG * KC * KE], F16)
        qst = sb("qst", [P, NG, T], F16)
        qbd = sb("qbd", [P, 2, ROWS], F16)
        h16 = k16[:, :, :].rearrange("p a n -> p (a n)")[:, 0:T]
        l16 = kT16[:, :, :].rearrange("p a n -> p (a n)")[:, 0:T]
        mx = sb("mx", [P, 2, TH])
        negmax = sb("negmax", [P, 2])
        rowsum = sb("rowsum", [P, 2, TILES])
        rs16 = sb("rs16", [P, 2, TILES], F16)
        rsel = sb("rsel", [P, 2, TILES, S], F16)
        o_mask = sb("o_mask", [P, GH, S])
        o_sum = sb("o_sum", [P, S])
        r_inv = sb("r_inv", [P, S])
        comb = sb("comb", [P, S])
        wout_sb = sb("wout_sb", [P, D])
        id_sb = sb("id_sb", [P, P])
        id16_sb = sb("id16_sb", [P, P], F16)
        diag4_sb = sb("diag4_sb", [P, GH])
        diag4h_sb = sb("diag4h_sb", [P, GH], F16)
        rowq_sb = sb("rowq_sb", [P, TILES, S], F16)
        rowhead_sb = sb("rowhead_sb", [P, TILES, P], F16)
        mean_sb = sb("mean_sb", [P, P])
        centre_sb = sb("centre_sb", [P, P])
        std = sb("std", [P, 2, TT])
        rank_sb = sb("rank_sb", [P, E])
        gates_in = sb("gates_in", [P, 4])
        gates = sb("gates", [P, 4])
        scale_sb = sb("scale_sb", [P, 1])
        eps_sb = sb("eps_sb", [P, 1])
        rw_sb = sb("rw_sb", [P, 2, E])
        rb_sb = sb("rb_sb", [P, 2, E])
        w10_sb = sb("w10_sb", [P, E, F0])
        w20_sb = sb("w20_sb", [P, E // 2, D])
        B1R = E // 2 + E * F1 // P
        b1_rows = sb("b1_rows", [B1R, P])
        b1T = sb("b1T", [P, B1R])
        b10_sb = b1T[:, 0:E // 2]
        b11_sb = b1T[:, E // 2:B1R].rearrange("p (e k) -> p e k", e=E)
        b2_sb = sb("b2_sb", [E, 2, D])
        bias_flat = bias_sb[:, :, :].rearrange("p a n -> p (a n)")
        w11_sb = bias_flat[:, 0:E * F1].rearrange("p (e f) -> p e f", e=E)
        w21_sb = bias_flat[:, E * F1:2 * E * F1].rearrange("p (e k d) -> p e k d", e=E, k=F1 // P)
        ptX = sb("ptX", [P, KC * P])
        sel0_sb = ptX[0:E, 0:P * (E // 2)].rearrange("e (i p) -> e i p", p=P)
        sel1_sb = ptX[0:E, P * (E // 2):P * (E // 2 + E)].rearrange("e (i p) -> e i p", p=P)
        rt = [sb(f"rt{i}", [P, TT, E]) for i in range(4)]
        rm = sb("rm", [P, 4, TT])
        wT = sc[:, :, :].rearrange("p a n -> p (a n)")[0:E, 0:T]
        sq = ptT[:, 0:T]
        diag = ptT[:, T:2 * T]
        mix = ptT[:, 2 * T:2 * T + 12 * TQ].rearrange("p (s n) -> p s n", n=TQ)
        k2T = ptT[:, 0:4 * S2].rearrange("p (r u n) -> p r u n", r=2, u=2)
        p2T = ptT[:, 4 * S2:4 * S2 + KC * P].rearrange("p (c n) -> p c n", n=P)
        kst_f = kst[:, :, :].rearrange("p a n -> p (a n)").bitcast(F32)
        kv2 = [[kv[:, 0, :], kv[:, 1, :]], [kst_f[:, 0:KC * D], kst_f[:, KC * D:2 * KC * D]]]
        q2 = sb("q2", [P, 2, 2, HALF])
        o2 = sb("o2", [P, D])
        r2 = sb("r2", [P, 1])
        xin = sc[:, :, :].rearrange("p a n -> p (a n)")[:, 0:T].rearrange("p (i d) -> p i d", d=D)

        ps_s = stack.enter_context(nc.psum_tensor("ps_s", [P, TH, BANK], F32))
        ps_t = stack.enter_context(nc.psum_tensor("ps_t", [P, TH, BANK], F32))
        ps_o = stack.enter_context(nc.psum_tensor("ps_o", [P, BANK], F32))
        ps_m = stack.enter_context(nc.psum_tensor("ps_m", [P, BANK], F32))
        ps_kt = ps_m[:, :].bitcast(F16).rearrange("p (a n) -> p a n", a=2)
        pv_acc = ps_o[:, 0:GR]
        r_acc = ps_o[:, 256:256 + S]

        passed = sem("passed")
        early_in = sem("early_in")
        consts_in = sem("consts_in")
        x_in = sem("x_in")
        bias_in = sem("bias_in")
        xT_raw = sem("xT_raw")
        xT_done = sem("xT_done")
        b1_raw = sem("b1_raw")
        b1_done = sem("b1_done")
        eps_set = sem("eps_set")
        gates_done = sem("gates_done")
        ln_cent = sem("ln_cent")
        ln_sq = sem("ln_sq")
        ln_out = sem("ln_out")
        ln_var = sem("ln_var")
        ln_std = sem("ln_std")
        ln_inv = sem("ln_inv")
        ln_diag = sem("ln_diag")
        ln_spread = sem("ln_spread")
        ln_done = sem("ln_done")
        q_high = sem("q_high")
        q_low = sem("q_low")
        qst_in = sem("qst_in")
        keys_in = [sem(f"keys_in{w}") for w in range(RING)]
        late_in = sem("late_in")
        k_zero = sem("k_zero")
        k_high = sem("k_high")
        k_low = sem("k_low")
        kt_raw = sem("kt_raw")
        kt_done = sem("kt_done")
        kst_in = sem("kst_in")
        q_ready = sem("q_ready")
        scored = sem("scored")
        biased = sem("biased")
        negmaxed = sem("negmaxed")
        probs = sem("probs")
        t_raw = sem("t_raw")
        t_act = sem("t_act")
        t_dve = sem("t_dve")
        rs_part = sem("rs_part")
        rsel_done = sem("rsel_done")
        values_used = sem("values_used")
        attended = sem("attended")
        comb_step = sem("comb_step")
        combined = sem("combined")
        projected = sem("projected")
        updated = sem("updated")
        logits = sem("logits")
        route_step = sem("route_step")
        route_exp = sem("route_exp")
        routed = sem("routed")
        wT_raw = sem("wT_raw")
        wT_done = sem("wT_done")
        hidden0 = sem("hidden0")
        spread0 = sem("spread0")
        gelu_done = sem("gelu_done")
        weighted = sem("weighted")
        y_part = sem("y_part")
        mixed0 = sem("mixed0")
        w1_in = sem("w1_in")
        hidden1 = sem("hidden1")
        hid_act = sem("hid_act")
        hid_dve = sem("hid_dve")
        spread1 = sem("spread1")
        spread_out = sem("spread_out")
        b2_sum = sem("b2_sum")
        acc_set = sem("acc_set")
        y_done = sem("y_done")
        y_mul = sem("y_mul")
        y_add = sem("y_add")
        mixed1 = sem("mixed1")
        ctx2_in = [[sem(f"ctx2_in{r}{u}") for u in range(2)] for r in range(2)]
        q2_zero = sem("q2_zero")
        q2_done = sem("q2_done")
        t2_raw = sem("t2_raw")
        e2_act = sem("e2_act")
        e2_dve = sem("e2_dve")
        scored2 = sem("scored2")
        negmax2 = sem("negmax2")
        probs2 = sem("probs2")
        pv2 = sem("pv2")
        inv2 = sem("inv2")
        normal2 = sem("normal2")
        o2_raw = sem("o2_raw")
        updated2 = sem("updated2")
        out_raw = sem("out_raw")
        out_sb = sem("out_sb")
        stored = sem("stored")

        early = [(id_sb[:, :], ident), (mean_sb[:, :], mean_w), (centre_sb[:, :], centre_w)]
        consts = [
            (id16_sb[:, :], ident16), (diag4_sb[:, :], diag4), (diag4h_sb[0:ST, :], diag4h), (rowq_sb[:, :, :], row_q),
            (rowhead_sb[:, :, :], row_head), (wout_sb[:, :], w_out),
            (gates_in[:, 0:2], g_xattn.partition_broadcast(P)), (gates_in[:, 2:4], g_ffn.partition_broadcast(P)),
            (scale_sb[:, :], scale1.partition_broadcast(P)),
            (rank_sb[:, :], rank),
            (rw_sb[:, 0, :], r_w0), (rw_sb[:, 1, :], r_w1),
            (rb_sb[:, 0, :], r_b0.partition_broadcast(P)), (rb_sb[:, 1, :], r_b1.partition_broadcast(P)),
            (w10_sb[:, :, :], w1_0.rearrange("e d f -> d e f")),
            (w20_sb[:, :, :], w2_0.rearrange("(i e) f d -> (e f) i d", e=2)),
            (b1_rows[0:E // 2, :], b1_0.rearrange("(i e) f -> i (e f)", e=2)),
            (b1_rows[E // 2:B1R, :], b1_1.rearrange("e (k p) -> (e k) p", p=P)),
            (b2_sb[:, 0, :], b2_0), (b2_sb[:, 1, :], b2_1),
        ]
        CONSTS = 16 * len(consts)
        ctx_v = ctx_.rearrange("b (c p) d -> b p c d", p=KP)
        bias_v = bias.rearrange("a h q k -> (a h q) k").rearrange("(t p) k -> p t k", p=P)

        def third(j):
            return slice(CT * D * j, CT * D * (j + 1))

        def transposed(u, t, q):
            if u == 1 and t == 0:
                return ptX[0:KP, CT * P * q:CT * P * (q + 1)].rearrange("p (c r) -> p c r", r=P)
            return ptT[0:KP, :].rearrange("p (c r) -> p c r", r=ROWS)[:, CT * q:CT * (q + 1), P * t:P * (t + 1)]

        def ahead(b, w, k, d):
            return b + d, (w + d) % RING, k + (w + d) // RING

        NORM_IN = [(xT_done, NQ), (updated, B), (mixed0, NQ), (updated2, B // 2)]

        def chunk(c):
            return slice(TQ * c, TQ * (c + 1))

        def norm_cols(c):
            return slice(BANK * c, min(BANK * (c + 1), T))

        def centred(c):
            bank = ps_s[:, c, :] if c < TH else ps_t[:, 0, :]
            return bank[:, 0:min(BANK, T - BANK * c)]

        def spread_std(c):
            return (ps_t[:, 1, :], ps_t[:, 2, :], ps_o[:, :], ps_m[:, :])[c][:, 0:min(BANK, T - BANK * c)]

        variances = ps_m[:, BANK - TT:BANK]

        def norm_tensor(pe, r):
            sem_in, n_in = NORM_IN[r]
            pe.wait_ge(sem_in, n_in)
            for c in range(NQ):
                pe.matmul(centred(c), centre_sb[:, :], resid[:, norm_cols(c)], start=True, stop=True).then_inc(ln_cent, 1)
            for i in range(TT):
                if i % 4 == 0:
                    pe.wait_ge(ln_sq, NQ * r + i // 4 + 1)
                last = pe.matmul(variances[:, i:i + 1], sq[:, P * i:P * (i + 1)], mean_sb[:, 0:1], start=True, stop=True)
            last.then_inc(ln_var, 1)
            for c in range(NQ):
                pe.wait_ge(ln_diag, TT * r + min(4 * (c + 1), TT))
                pe.matmul(spread_std(c), mean_sb[:, :], diag[:, norm_cols(c)], start=True, stop=True).then_inc(ln_spread, 1)

        def norm_scalar(act, r):
            for c in range(NQ):
                act.wait_ge(ln_out, NQ * r + c + 1)
                act.activation(sq[:, norm_cols(c)], normed[:, norm_cols(c)], ACT.Square).then_inc(ln_sq, 1)
            act.wait_ge(eps_set, 1)
            act.wait_ge(ln_var, r + 1)
            act.activation(std[:, 0, :], variances, ACT.Sqrt, bias=eps_sb[:, 0:1], scale=1.0 / D ** 2).then_inc(ln_std, 1)

        def norm_vector(dve, r):
            for c in range(NQ):
                dve.wait_ge(ln_cent, NQ * r + c + 1)
                dve.tensor_copy(normed[:, norm_cols(c)], centred(c)).then_inc(ln_out, 1)
            dve.wait_ge(ln_std, r + 1)
            dve.reciprocal(std[:, 1, :], std[:, 0, :]).then_inc(ln_inv, 1)
            dve.wait_ge(ln_inv, r + 1)
            for i in range(TT):
                dve.tensor_scalar(diag[:, P * i:P * (i + 1)], id_sb[:, :], std[:, 1, i:i + 1], None, ALU.mult).then_inc(ln_diag, 1)
            for c in range(NQ):
                dve.wait_ge(ln_out, NQ * r + c + 1)
                dve.wait_ge(ln_spread, NQ * r + c + 1)
                dve.tensor_tensor(normed[:, norm_cols(c)], normed[:, norm_cols(c)], spread_std(c), ALU.mult).then_inc(ln_done, 1)

        def four_tiles(i):
            bank = ps_s[:, i // 4, :] if i < 4 * TH else ps_t[:, 0, :]
            return bank[:, P * (i % 4):P * (i % 4 + 1)]

        def route_tensor(pe, layer):
            pe.wait_ge(ln_done, NQ * (2 * layer + 2))
            for i in range(TT):
                last = pe.matmul(ps_o[:, E * i:E * (i + 1)], normed[:, P * i:P * (i + 1)], rw_sb[:, layer, :], start=True, stop=True)
            last.then_inc(logits, 1)
            pe.wait_ge(routed, layer + 1)
            for i in range(TT):
                last = pe.transpose(four_tiles(i)[0:E, :], rt[2][:, i, :], id_sb[:, :])
            last.then_inc(wT_raw, 1)

        def route_scalar(act, layer):
            act.wait_ge(route_step, ROUTE_STEPS * layer + ROUTE_EXP)
            act.activation(rm[:, 3, :], rm[:, 2, :], ACT.Exp).then_inc(route_exp, 1)

        def route_vector(dve, layer):
            step = [ROUTE_STEPS * layer]

            def link(instruction):
                step[0] += 1
                instruction.then_inc(route_step, 1)
                dve.wait_ge(route_step, step[0])

            def per_token(v):
                return v.unsqueeze(2).broadcast_to([P, TT, E])

            def one_hot(dst, src, top):
                link(dve.tensor_reduce(rm[:, top, :], src[:, :, :], axis=AX.X, op=ALU.max))
                link(dve.tensor_tensor(dst[:, :, :], src[:, :, :], per_token(rm[:, top, :]), ALU.is_equal))
                link(dve.tensor_tensor(dst[:, :, :], dst[:, :, :], rank_sb[:, :].unsqueeze(1).broadcast_to([P, TT, E]), ALU.mult))
                link(dve.tensor_reduce(rm[:, 1, :], dst[:, :, :], axis=AX.X, op=ALU.max))
                link(dve.tensor_tensor(dst[:, :, :], dst[:, :, :], per_token(rm[:, 1, :]), ALU.is_equal))

            dve.wait_ge(logits, layer + 1)
            link(dve.tensor_tensor(rt[0][:, :, :], ps_o[:, 0:TT * E].rearrange("p (i e) -> p i e", e=E),
                                   rb_sb[:, layer, :].unsqueeze(1).broadcast_to([P, TT, E]), ALU.add))
            one_hot(rt[1], rt[0], 0)
            link(dve.scalar_tensor_tensor(out=rt[2][:, :, :], in0=rt[1][:, :, :], scalar=-3.0e38, in1=rt[0][:, :, :],
                                          op0=ALU.mult, op1=ALU.add))
            one_hot(rt[3], rt[2], 2)
            link(dve.tensor_tensor(rm[:, 2, :], rm[:, 2, :], rm[:, 0, :], ALU.subtract))
            assert step[0] == ROUTE_STEPS * layer + ROUTE_EXP
            dve.wait_ge(route_exp, layer + 1)
            link(dve.tensor_scalar(rm[:, 0, :], rm[:, 3, :], 1.0, None, ALU.add))
            link(dve.reciprocal(rm[:, 1, :], rm[:, 0, :]))
            link(dve.tensor_tensor(rm[:, 2, :], rm[:, 3, :], rm[:, 1, :], ALU.mult))
            link(dve.tensor_tensor(rt[1][:, :, :], rt[1][:, :, :], per_token(rm[:, 1, :]), ALU.mult))
            link(dve.tensor_tensor(rt[3][:, :, :], rt[3][:, :, :], per_token(rm[:, 2, :]), ALU.mult))
            assert step[0] == ROUTE_STEPS * (layer + 1)
            dve.tensor_tensor(rt[2][:, :, :], rt[1][:, :, :], rt[3][:, :, :], ALU.add).then_inc(routed, 1)
            dve.wait_ge(wT_raw, layer + 1)
            for c in range(NQ):
                n = min(4 * P, T - 4 * P * c)
                bank = ps_s[:, c, :] if c < TH else ps_t[:, 0, :]
                dve.tensor_copy(wT[:, 4 * P * c:4 * P * c + n], bank[0:E, 0:n]).then_inc(wT_done, 1)

        PAIRS = E // 2

        def y0_bank(c):
            return (ps_o if c % 2 else ps_m)[:, 0:TQ]

        def mixture0_tensor(pe):
            route_tensor(pe, 0)
            pe.wait_ge(late_in, 32)
            pe.wait_ge(wT_done, NQ)

            def output(k):
                c, i = divmod(k, PAIRS)
                if i == 0:
                    if c >= 2:
                        pe.wait_ge(mixed0, c - 1)
                    pe.matmul(y0_bank(c), b2_sb[:, 0, :], wT[:, chunk(c)], start=True, stop=False)
                pe.wait_ge(weighted, k + 1)
                pe.matmul(y0_bank(c), w20_sb[:, i, :], mix[:, 2 + k % 2, :], start=False, stop=i == PAIRS - 1).then_inc(y_part, 1)

            for k in range(NQ * PAIRS):
                c, i = divmod(k, PAIRS)
                if k >= 2:
                    pe.wait_ge(gelu_done, k - 1)
                pe.matmul(ps_s[:, k % 2, 0:TQ], w10_sb[:, 2 * i:2 * i + 2, :].rearrange("p e f -> p (e f)"),
                          normed[:, chunk(c)], start=True, stop=True).then_inc(hidden0, 1)
                if k >= 2:
                    pe.wait_ge(weighted, k - 1)
                pe.matmul(ps_t[:, k % 2, 0:TQ], sel0_sb[:, i, :], wT[:, chunk(c)], start=True, stop=True).then_inc(spread0, 1)
                if k >= 1:
                    output(k - 1)
            output(NQ * PAIRS - 1)

        def mixture0_scalar(act):
            route_scalar(act, 0)
            for k in range(NQ * PAIRS):
                act.wait_ge(hidden0, k + 1)
                if k >= 2:
                    act.wait_ge(weighted, k - 1)
                act.activation(mix[:, k % 2, :], ps_s[:, k % 2, 0:TQ], ACT.Gelu, bias=b10_sb[:, k % PAIRS:k % PAIRS + 1]).then_inc(gelu_done, 1)

        def mixture0_vector(dve):
            route_vector(dve, 0)
            for k in range(NQ * PAIRS):
                c, i = divmod(k, PAIRS)
                dve.wait_ge(gelu_done, k + 1)
                dve.wait_ge(spread0, k + 1)
                if k >= 2:
                    dve.wait_ge(y_part, k - 1)
                dve.tensor_tensor(mix[:, 2 + k % 2, :], mix[:, k % 2, :], ps_t[:, k % 2, 0:TQ], ALU.mult).then_inc(weighted, 1)
                if i == PAIRS - 1:
                    dve.wait_ge(y_part, k + 1)
                    dve.scalar_tensor_tensor(out=resid[:, chunk(c)], in0=y0_bank(c), scalar=gates[:, 2:3], in1=resid[:, chunk(c)],
                                             op0=ALU.mult, op1=ALU.add).then_inc(mixed0, 1)

        NP2 = B // 2

        def pairs(eng, pair):
            pair(0, 0, 0)
            with eng.Fori(0, (NP2 - 2) // 2) as i:
                pair(2 * i + 1, 1, i)
                pair(2 * i + 2, 0, i + 1)
            pair(NP2 - 1, 1, NP2 // 2 - 1, last=True)

        def act_before(p):
            return 6 * p + 4

        def dve_before(p):
            return 3 * p + 2

        def turned_before(p):
            return 0 if isinstance(p, int) and p == 0 else 9 * p - 3

        def second_attention_sync(sp):
            def load(p, r):
                for u in range(2):
                    sp.dma_start(kv2[r][u][0:KP, :].rearrange("p (c d) -> p c d", d=D),
                                 ctx_v[bass.ds(2 * p + u, 1), :, :, :].rearrange("a p c d -> p (a c) d")).then_inc(ctx2_in[r][u], 16)

            sp.wait_ge(attended, B)
            for dst, src in ((sel0_sb, sel0), (sel1_sb, sel1)):
                sp.dma_start(dst, src).then_inc(late_in, 16)
            load(0, 0)
            for dst, src in ((w11_sb, w1_1.rearrange("e d f -> d e f")),
                             (w21_sb, w2_1.rearrange("e (k p) d -> p e k d", p=P))):
                sp.dma_start(dst, src).then_inc(w1_in, 16)

            def pair(p, r, k, last=False):
                if not last:
                    if not isinstance(p, int) or p > 0:
                        sp.wait_ge(pv2, p)
                        sp.sem_inc(passed, 1)
                    load(p + 1, 1 - r)

            pairs(sp, pair)
            for c in range(NQ):
                n = min(4, TT - 4 * c)
                sp.wait_ge(out_sb, c + 1)
                sp.dma_start(out.rearrange("b s d -> (b s) d")[4 * P * c:4 * P * c + P * n, :].rearrange("(i p) d -> p i d", p=P),
                             xin[:, 4 * c:4 * c + n, :]).then_inc(stored, 16)
            sp.wait_ge(stored, 16 * NQ)

        def second_attention_pool(pool):
            pool.wait_ge(ln_done, NQ * 3)
            pool.memset(q2[:, :, :, :], 0.0).then_inc(q2_zero, 1)
            pool.wait_ge(q2_zero, 1)

            def queries(p, r):
                pool.tensor_tensor(q2[:, r, :, 0:S], normed[:, bass.ds(2 * S * p, 2 * S)].rearrange("p (u q) -> p u q", u=2),
                                   scale_sb[:, 0:1].unsqueeze(2).broadcast_to([P, 2, S]), ALU.mult).then_inc(q2_done, 1)

            queries(0, 0)

            def pair(p, r, k, last=False):
                if not last:
                    if not isinstance(p, int) or p > 0:
                        pool.wait_ge(scored2, p)
                    queries(p + 1, 1 - r)

            pairs(pool, pair)

        def second_attention_scalar(act):
            def keys_out(p, r):
                for u in range(2):
                    for j in range(2):
                        act.wait_ge(t2_raw, turned_before(p) + TH * u + j + 1)
                        act.activation(k2T[:, r, u, KT * j:KT * (j + 1)], ps_t[:, j, 0:KT], ACT.Copy).then_inc(e2_act, 1)

            act.wait_ge(ln_done, NQ * 3)
            keys_out(0, 0)

            def pair(p, r, k, last=False):
                act.wait_ge(negmax2, p + 1)
                act.activation(sc[:, r, :].rearrange("p (j n) -> p j n", j=TH), ps_s[:, :, 0:KT], ACT.Exp, bias=negmax[:, 0:1],
                               accum_out=rowsum[:, 0, 0:1]).then_inc(probs2, 1)
                if not last:
                    keys_out(p + 1, 1 - r)
                for q in range(2):
                    act.wait_ge(t2_raw, 9 * p + (6 if last else 12) + q + 1)
                    act.activation(p2T[0:KP, CT * q:CT * (q + 1), :], ps_t[0:KP, q, :].rearrange("p (c n) -> p c n", n=P),
                                   ACT.Copy).then_inc(e2_act, 1)

            pairs(act, pair)

        def second_attention_vector(dve):
            def keys_out(p, r):
                for u in range(2):
                    dve.wait_ge(t2_raw, turned_before(p) + TH * u + TH)
                    dve.tensor_copy(k2T[:, r, u, 2 * KT:3 * KT], ps_t[:, 2, 0:KT]).then_inc(e2_dve, 1)

            def update(p):
                dve.wait_ge(o2_raw, p + 1)
                r = resid[:, bass.ds(2 * S * p, 2 * S)].rearrange("p (u q) -> p u q", u=2)
                dve.scalar_tensor_tensor(out=r, in0=ps_m[:, 0:P].rearrange("p (u q) -> p u q", u=2)[:, :, 0:S],
                                         scalar=gates[:, 1:2], in1=r, op0=ALU.mult, op1=ALU.add).then_inc(updated2, 1)

            keys_out(0, 0)

            def pair(p, r, k, last=False):
                dve.wait_ge(scored2, p + 1)
                dve.tensor_reduce(negmax[:, 0:1], ps_s[:, :, 0:KT], axis=AX.XY, op=ALU.max, negate=True).then_inc(negmax2, 1)
                if not isinstance(p, int) or p > 0:
                    update(p - 1)
                if not last:
                    keys_out(p + 1, 1 - r)
                dve.wait_ge(t2_raw, 9 * p + (9 if last else 15))
                dve.tensor_copy(p2T[0:KP, 2 * CT:3 * CT, :], ps_t[0:KP, 2, :].rearrange("p (c n) -> p c n", n=P)).then_inc(e2_dve, 1)
                dve.wait_ge(probs2, p + 1)
                dve.reciprocal(r2[:, 0:1], rowsum[:, 0, 0:1]).then_inc(inv2, 1)
                dve.wait_ge(inv2, p + 1)
                dve.wait_ge(pv2, p + 1)
                if not isinstance(p, int) or p > 0:
                    dve.wait_ge(o2_raw, p)
                dve.tensor_scalar(o2[:, :], ps_o[:, 0:D], r2[:, 0:1], None, ALU.mult).then_inc(normal2, 1)

            pairs(dve, pair)
            update(NP2 - 1)

        def second_attention_tensor(pe):
            def keys(p, r, k):
                for u in range(2):
                    pe.wait_ge(ctx2_in[r][u], 16 * (k + 1))
                    for j in range(TH):
                        if not isinstance(p, int) or p > 0:
                            if j < 2:
                                pe.wait_ge(e2_act, act_before(p - 1) - 2 + 2 * u + j + 1)
                            else:
                                pe.wait_ge(e2_dve, dve_before(p - 1) + u)
                        elif u == 1:
                            if j < 2:
                                pe.wait_ge(e2_act, j + 1)
                            else:
                                pe.wait_ge(e2_dve, 1)
                        for c in range(CT):
                            cc = CT * j + c
                            last = pe.transpose(ps_t[:, j, KP * c:KP * (c + 1)], kv2[r][u][0:KP, D * cc:D * (cc + 1)], id_sb[0:KP, 0:KP])
                        last.then_inc(t2_raw, 1)

            def turn_output(p):
                pe.wait_ge(normal2, p + 1)
                pe.transpose(ps_m[:, 0:P], o2[:, :], id_sb[:, :]).then_inc(o2_raw, 1)

            pe.wait_ge(ln_done, NQ * 3)
            keys(0, 0, 0)

            def pair(p, r, k, last=False):
                pe.wait_ge(q2_done, p + 1)
                pe.wait_ge(e2_act, act_before(p) - (2 if not isinstance(p, int) or p > 0 else 0))
                pe.wait_ge(e2_dve, dve_before(p))
                if not isinstance(p, int) or p > 0:
                    pe.wait_ge(probs2, p)
                for j in range(TH):
                    for u in range(2):
                        last_mm = pe.matmul(ps_s[HALF * u:HALF * (u + 1), j, 0:KT], q2[:, r, u, :], k2T[:, r, u, KT * j:KT * (j + 1)],
                                            start=True, stop=True)
                last_mm.then_inc(scored2, 1)
                if not isinstance(p, int) or p > 0:
                    turn_output(p - 1)
                if not last:
                    keys(p + 1, 1 - r, k + r)
                pe.wait_ge(probs2, p + 1)
                for q in range(TH):
                    if q < 2:
                        pe.wait_ge(e2_act, act_before(p) + (-2 if last else 2) + q + 1)
                    else:
                        pe.wait_ge(e2_dve, dve_before(p) + (0 if last else 2))
                    for c in range(CT):
                        cc = CT * q + c
                        last_mm = pe.transpose(ps_t[0:KP, q, P * c:P * (c + 1)], sc[:, r, KP * cc:KP * (cc + 1)], id_sb[:, :])
                    last_mm.then_inc(t2_raw, 1)
                pe.wait_ge(e2_act, act_before(p) + (2 if last else 6))
                pe.wait_ge(e2_dve, dve_before(p) + (1 if last else 3))
                if not isinstance(p, int) or p > 0:
                    pe.wait_ge(normal2, p)
                for c in range(KC):
                    for u in range(2):
                        last_mm = pe.matmul(ps_o[HALF * u:HALF * (u + 1), 0:D], p2T[0:KP, c, HALF * u:HALF * (u + 1)],
                                            kv2[r][u][0:KP, D * c:D * (c + 1)], start=c == 0, stop=c == KC - 1)
                last_mm.then_inc(pv2, 1)

            pairs(pe, pair)
            turn_output(NP2 - 1)

        FK = F1 // P

        def chunks(eng, body):
            body(0, first=True)
            with eng.Fori(1, NQ) as c:
                body(c)

        def tokens(c):
            return bass.ds(TQ * c, TQ)

        def hidden_bank(f):
            return (ps_s[:, f, 0:TQ] if f < TH else ps_t[:, 0, 0:TQ])

        def y1_bank(e):
            return (ps_o if e % 2 else ps_m)[:, 0:TQ]

        def mixture1_tensor(pe):
            route_tensor(pe, 1)
            pe.wait_ge(wT_done, 2 * NQ)
            pe.wait_ge(w1_in, 32)

            def output(k, e, f):
                if f == 0 and (not isinstance(k, int) or k >= 2):
                    pe.wait_ge(y_mul, k - 1)
                pe.wait_ge(hid_dve if f % 2 else hid_act, FK // 2 * k + f // 2 + 1)
                last = pe.matmul(y1_bank(e), w21_sb[:, e, f, :], mix[:, FK * (e % 2) + f, :], start=f == 0, stop=f == FK - 1)
                if f == FK - 1:
                    last.then_inc(y_done, 1)

            def body(c, first=False):
                for e in range(E):
                    k = E * c + e
                    start = first and e == 0
                    for f in range(FK):
                        if not start:
                            pe.wait_ge(hid_dve if f % 2 else hid_act, FK // 2 * (k - 1) + f // 2 + 1)
                        pe.matmul(hidden_bank(f), w11_sb[:, e, P * f:P * (f + 1)], normed[:, tokens(c)], start=True, stop=True).then_inc(hidden1, 1)
                        if not start:
                            output(k - 1, (e - 1) % E, f)
                    if not start:
                        pe.wait_ge(spread_out, k)
                        pe.sem_inc(passed, 1)
                    pe.matmul(ps_t[:, 1, 0:TQ], sel1_sb[:, e, :], wT[:, tokens(c)], start=True, stop=True).then_inc(spread1, 1)
                    if e == 0:
                        if not first:
                            pe.wait_ge(acc_set, c)
                            pe.sem_inc(passed, 1)
                        pe.matmul(ps_t[:, 2, 0:TQ], b2_sb[:, 1, :], wT[:, tokens(c)], start=True, stop=True).then_inc(b2_sum, 1)

            chunks(pe, body)
            for f in range(FK):
                output(E * NQ - 1, E - 1, f)
            pe.wait_ge(mixed1, NQ)
            for i in range(TT):
                last = pe.transpose(four_tiles(i), resid[:, P * i:P * (i + 1)], id_sb[:, :])
                if i % 4 == 3 or i == TT - 1:
                    last.then_inc(out_raw, 1)

        def mixture1_scalar(act):
            route_scalar(act, 1)

            def body(c, first=False):
                for e in range(E):
                    k = E * c + e
                    for f in range(0, FK, 2):
                        act.wait_ge(hidden1, FK * k + f + 1)
                        if not isinstance(k, int) or k >= 2:
                            act.wait_ge(y_done, k - 1)
                        act.activation(mix[:, FK * (e % 2) + f, :], hidden_bank(f), ACT.Relu, bias=b11_sb[:, e, f:f + 1]).then_inc(hid_act, 1)
                    act.wait_ge(spread1, k + 1)
                    if not isinstance(k, int) or k >= 2:
                        act.wait_ge(y_mul, k - 1)
                    act.activation(mix[:, 2 * FK + e % 2, :], ps_t[:, 1, 0:TQ], ACT.Copy).then_inc(spread_out, 1)

            chunks(act, body)

        def mixture1_vector(dve):
            route_vector(dve, 1)
            prod, total = mix[:, 2 * FK + 2, :], mix[:, 2 * FK + 3, :]

            def weigh(k, e):
                dve.wait_ge(y_done, k + 1)
                dve.wait_ge(spread_out, k + 1)
                if not isinstance(k, int) or k >= 1:
                    dve.wait_ge(y_add, k)
                dve.tensor_tensor(prod, y1_bank(e), mix[:, 2 * FK + e % 2, :], ALU.mult).then_inc(y_mul, 1)
                dve.wait_ge(y_mul, k + 1)
                dve.tensor_tensor(total, total, prod, ALU.add).then_inc(y_add, 1)

            def finish(c):
                dve.wait_ge(y_add, E * (c + 1))
                r = resid[:, tokens(c)]
                dve.scalar_tensor_tensor(out=r, in0=total, scalar=gates[:, 3:4], in1=r, op0=ALU.mult, op1=ALU.add).then_inc(mixed1, 1)

            def body(c, first=False):
                for e in range(E):
                    k = E * c + e
                    for f in range(1, FK, 2):
                        dve.wait_ge(hidden1, FK * k + f + 1)
                        if not isinstance(k, int) or k >= 2:
                            dve.wait_ge(y_done, k - 1)
                        dve.tensor_scalar(mix[:, FK * (e % 2) + f, :], hidden_bank(f), b11_sb[:, e, f:f + 1], 0.0,
                                          ALU.add, ALU.max).then_inc(hid_dve, 1)
                    if not (first and e == 0):
                        weigh(k - 1, (e - 1) % E)
                    if e == 0:
                        if not first:
                            finish(c - 1)
                            dve.wait_ge(mixed1, c)
                        dve.wait_ge(b2_sum, c + 1)
                        dve.tensor_copy(total, ps_t[:, 2, 0:TQ]).then_inc(acc_set, 1)
                        dve.wait_ge(acc_set, c + 1)

            chunks(dve, body)
            weigh(E * NQ - 1, E - 1)
            finish(NQ - 1)
            for c in range(NQ):
                n = min(4, TT - 4 * c)
                dve.wait_ge(out_raw, c + 1)
                bank = ps_s[:, c, :] if c < TH else ps_t[:, 0, :]
                dve.tensor_copy(xin[:, 4 * c:4 * c + n, :].rearrange("p i d -> p (i d)"), bank[:, 0:P * n]).then_inc(out_sb, 1)

        block = stack.enter_context(nc.Block())

        def batches(eng, batch):
            batch(0, 0, 0, 2, first=True)
            with eng.Fori(0, B // RING - 1) as i:
                for d in range(1, RING + 1):
                    batch(RING * i + d, d % RING, i + d // RING, 2)
            for left in (2, 1, 0):
                batch(B - 1 - left, RING - 1 - left, B // RING - 1, left)

        @block.sync
        def _(sp):
            def load_keys(b, w):
                sp.dma_start(ring[w][0:KP, :].rearrange("p (c d) -> p c d", d=D),
                             ctx_v[bass.ds(b, 1), :, :, :].rearrange("a p c d -> p (a c) d")).then_inc(keys_in[w], 16)

            def stack_keys(b, u):
                sp.wait_ge(kt_done, TH * (b + 1))
                if not isinstance(b, int) or b > 1:
                    if not isinstance(b, int):
                        sp.sem_inc(passed, 1)
                    sp.wait_ge(scored, TH * TILES * (b - 1))
                for term, half in enumerate((0, 0, 1)):
                    for g in range(NG):
                        sp.dma_start(kst[GD * term:GD * (term + 1), u, KTE * TH * g:KTE * TH * (g + 1)],
                                     kT16[GD * g:GD * (g + 1), half, :]).then_inc(kst_in, 16)

            for dst, src in early:
                sp.dma_start(dst, src).then_inc(early_in, 16)
            sp.dma_start(xin, x.rearrange("b s d -> (b s) d").rearrange("(i p) d -> p i d", p=P)).then_inc(x_in, 16)
            load_keys(0, 0)
            for dst, src in consts:
                sp.dma_start(dst, src).then_inc(consts_in, 16)
            sp.dma_start(bias_sb[:, :, :], bias_v).then_inc(bias_in, 16)
            for term, (half, ready) in enumerate(((h16, q_high), (l16, q_low), (h16, q_high))):
                sp.wait_ge(ready, 1)
                for g in range(NG):
                    sp.dma_start(qst[GD * term:GD * (term + 1), g, :], half[GD * g:GD * (g + 1), :]).then_inc(qst_in, 16)
            load_keys(1, 1)
            load_keys(2, 2)
            load_keys(3, 3)
            stack_keys(0, 0)

            stack_keys(1, 1)

            def batch(b, w, k, left):
                sp.wait_ge(values_used, b)
                if left == 2:
                    if not isinstance(b, int):
                        sp.sem_inc(passed, 1)
                    load_keys(b + RING - 1, (w - 1) % RING)
                stack_keys(b + 1, (w + 1) % 2)

            with sp.Fori(0, B // RING - 1) as i:
                for d in range(1, RING + 1):
                    batch(RING * i + d, d % RING, i, 2)
            stack_keys(B - 2, 0)
            stack_keys(B - 1, 1)
            second_attention_sync(sp)

        @block.gpsimd
        def _(pool):
            pool.wait_ge(consts_in, CONSTS)
            pool.wait_ge(ln_done, NQ)
            pool.wait_ge(q_high, 1)
            pool.tensor_tensor(l16, normed[:, :], h16, ALU.subtract).then_inc(q_low, 1)

            def low(b, w, j):
                pool.wait_ge(k_high, TH * b + j + 1)
                s = third(j)
                pool.tensor_tensor(k16[0:KP, 1, s], ring[w][0:KP, s], k16[0:KP, 0, s], ALU.subtract).then_inc(k_low, 1)

            def queries(b, u, first=False):
                if not first:
                    pool.wait_ge(scored, TH * TILES * (b - 1))
                for g in range(NG):
                    dst = qbd[0:ST, u, GR * g:GR * (g + 1)].rearrange("p (h q) -> p h q", h=GH)
                    q = qst[0:ST, g, bass.ds(S * b, S)].unsqueeze(1).broadcast_to([ST, GH, S])
                    m = diag4h_sb[0:ST, :].unsqueeze(2).broadcast_to([ST, GH, S])
                    done = pool.tensor_tensor(dst, q, m, ALU.mult)
                done.then_inc(q_ready, 1)

            def row_sums(b, u, first=False):
                pool.wait_ge(probs, TILES * (b + 1))
                if not first:
                    pool.wait_ge(attended, b)
                pool.sem_inc(passed, 1)
                pool.tensor_copy(rs16[:, 0, :], rowsum[:, u, :]).then_inc(rs_part, 1)
                pool.wait_ge(rs_part, 2 * b + 1)
                pool.tensor_tensor(rs16[:, 1, :], rowsum[:, u, :], rs16[:, 0, :], ALU.subtract).then_inc(rs_part, 1)
                pool.wait_ge(rs_part, 2 * b + 2)
                for half in range(2):
                    r = rs16[:, half, :].unsqueeze(2).broadcast_to([P, TILES, S])
                    done = pool.tensor_tensor(rsel[:, half, :, :], rowq_sb[:, :, :], r, ALU.mult)
                done.then_inc(rsel_done, 1)

            for j in range(TH):
                low(0, 0, j)
            pool.wait_ge(qst_in, STACKED)
            queries(0, 0, first=True)
            for j in range(TH):
                low(1, 1, j)

            def batch(b, w, k, left, first=False):
                u = w % 2
                if left > 0:
                    queries(b + 1, 1 - u, first=first)
                if left > 1:
                    for j in range(TH):
                        low(b + 2, (w + 2) % RING, j)
                row_sums(b, u, first=first)

            batches(pool, batch)
            second_attention_pool(pool)

        @block.scalar
        def _(act):
            act.wait_ge(consts_in, CONSTS)
            act.activation(gates[:, :], gates_in[:, :], ACT.Tanh).then_inc(gates_done, 1)
            norm_scalar(act, 0)
            act.wait_ge(ln_done, NQ)
            act.activation(h16, normed[:, :], ACT.Copy).then_inc(q_high, 1)

            def keys_out(b, j):
                act.wait_ge(kt_raw, TH * b + j + 1)
                if not isinstance(b, int) or b > 0:
                    act.wait_ge(kst_in, STACKED * b)
                act.activation(kT16[:, :, KTE * j:KTE * (j + 1)], ps_kt[:, :, 0:KTE], ACT.Copy).then_inc(kt_done, 1)

            def evacuate(n, u, t, q):
                act.wait_ge(t_raw, TH * n + q + 1)
                act.activation(transposed(u, t, q),
                               ps_t[0:KP, q, :].rearrange("p (c r) -> p c r", r=P), ACT.Copy).then_inc(t_act, 1)

            def exponent(n, s, t, u):
                act.wait_ge(negmaxed, n + 1)
                act.activation(sc[:, s, :], sc[:, s, :], ACT.Exp, bias=negmax[:, s:s + 1],
                               accum_out=rowsum[:, u, t:t + 1]).then_inc(probs, 1)

            def batch(b, w, k, left, first=False):
                u = w % 2
                for t in range(TILES):
                    n = TILES * b + t
                    if t == TILES - 1 and left > 0 and not first:
                        act.wait_ge(rsel_done, b)
                    before = (n - 1, u if t > 0 else 1 - u, (t - 1) % TILES)
                    if not (first and t == 0):
                        evacuate(*before, 0)
                    exponent(n, (u + t) % 2, t, u)
                    if not (first and t == 0):
                        evacuate(*before, 1)
                    if t == 0 and left > 0:
                        keys_out(b + 1, 2)
                    if t >= TILES - 2 and left > 1:
                        keys_out(b + 2, t - (TILES - 2))

            for j in range(TH):
                keys_out(0, j)
            for j in range(2):
                keys_out(1, j)
            batches(act, batch)
            evacuate(TILES * B - 1, 1, TILES - 1, 0)
            evacuate(TILES * B - 1, 1, TILES - 1, 1)
            norm_scalar(act, 1)
            mixture0_scalar(act)
            norm_scalar(act, 2)
            second_attention_scalar(act)
            norm_scalar(act, 3)
            mixture1_scalar(act)

        @block.vector
        def _(dve):
            dve.memset(eps_sb[:, :], EPS / D ** 2).then_inc(eps_set, 1)
            for c in range(NQ):
                n = min(4, TT - 4 * c)
                dve.wait_ge(xT_raw, c + 1)
                src = (ps_s[:, c, :] if c < TH else ps_t[:, 0, :])[:, 0:P * n]
                dve.tensor_copy(resid[:, 4 * P * c:4 * P * c + P * n], src).then_inc(xT_done, 1)
            dve.wait_ge(b1_raw, 1)
            dve.tensor_copy(b1T[:, :], ps_o[:, 0:B1R]).then_inc(b1_done, 1)
            norm_vector(dve, 0)

            def high(b, w, k, j):
                dve.wait_ge(keys_in[w], 16 * (k + 1))
                if not isinstance(b, int) or b > 0:
                    dve.wait_ge(kt_raw, TH * (b - 1) + j + 1)
                dve.tensor_copy(k16[0:KP, 0, third(j)], ring[w][0:KP, third(j)]).then_inc(k_high, 1)

            def bias_max(n, s, u, t, start=False):
                for j in range(TH):
                    if j == TH - 1 and not start:
                        evacuate(n - 2, u if t > 1 else 1 - u, (t - 2) % TILES)
                    dve.wait_ge(scored, TH * n + j + 1)
                    if not isinstance(n, int) or n >= 2:
                        dve.wait_ge(t_raw, TH * (n - 2) + j + 1)
                    dve.sem_inc(passed, 1)
                    dve.tensor_tensor_reduce(
                        out=sc[:, s, KT * j:KT * (j + 1)], in0=ps_s[:, j, 0:KT], in1=bias_sb[:, t, KT * j:KT * (j + 1)],
                        scale=SCALE0, scalar=-3.0e38, op0=ALU.add, op1=ALU.max,
                        accum_out=mx[:, s, j:j + 1]).then_inc(biased, 1)
                dve.wait_ge(biased, TH * (n + 1))
                dve.tensor_reduce(negmax[:, s:s + 1], mx[:, s, :], axis=AX.X, op=ALU.max,
                                  negate=True).then_inc(negmaxed, 1)

            def evacuate(n, u, t):
                dve.wait_ge(t_raw, TH * (n + 1))
                dve.tensor_copy(transposed(u, t, 2),
                                ps_t[0:KP, 2, :].rearrange("p (c r) -> p c r", r=P)).then_inc(t_dve, 1)

            def combine(b):
                dve.wait_ge(attended, b + 1)
                m = diag4_sb[:, :].unsqueeze(2).broadcast_to([P, GH, S])
                dve.tensor_tensor(o_mask[:, :, :], pv_acc.rearrange("p (h q) -> p h q", h=GH), m, ALU.mult).then_inc(comb_step, 1)
                dve.reciprocal(r_inv[:, :], r_acc).then_inc(comb_step, 1)
                dve.wait_ge(comb_step, 3 * b + 1)
                dve.tensor_reduce(o_sum[:, :], o_mask[:, :, :].rearrange("p h q -> p q h"), axis=AX.X, op=ALU.add
                                  ).then_inc(comb_step, 1)
                dve.wait_ge(comb_step, 3 * b + 3)
                dve.tensor_tensor(comb[:, :], o_sum[:, :], r_inv[:, :], ALU.mult).then_inc(combined, 1)

            def update(b):
                dve.wait_ge(projected, b + 1)
                r = resid[:, bass.ds(S * b, S)]
                dve.scalar_tensor_tensor(out=r, in0=ps_m[:, 0:S], scalar=gates[:, 0:1], in1=r,
                                         op0=ALU.mult, op1=ALU.add).then_inc(updated, 1)

            dve.wait_ge(qst_in, STACKED)
            dve.memset(k16[96:P, :, :], 0.0).then_inc(k_zero, 1)
            dve.wait_ge(k_zero, 1)
            for j in range(TH):
                high(0, 0, 0, j)
            for j in range(TH):
                high(1, 1, 0, j)
            dve.wait_ge(bias_in, 16)
            dve.wait_ge(gates_done, 1)

            def batch(b, w, k, left, first=False):
                u = w % 2
                for t in range(TILES):
                    n = TILES * b + t
                    bias_max(n, (u + t) % 2, u, t, start=first and t < 2)
                    if not first and t == 3:
                        combine(b - 1)
                    if not first and t == 4:
                        update(b - 1)
                    if left > 1 and t == 1:
                        for j in range(TH):
                            high(*ahead(b, w, k, 2), j)

            batches(dve, batch)
            evacuate(TILES * B - 2, 1, TILES - 2)
            evacuate(TILES * B - 1, 1, TILES - 1)
            combine(B - 1)
            update(B - 1)
            norm_vector(dve, 1)
            mixture0_vector(dve)
            norm_vector(dve, 2)
            second_attention_vector(dve)
            norm_vector(dve, 3)
            mixture1_vector(dve)

        @block.tensor
        def _(pe):
            pe.wait_ge(early_in, 16 * len(early))
            pe.wait_ge(x_in, 16)
            for i in range(TT):
                c = i // 4
                dst = (ps_s[:, c, :] if c < TH else ps_t[:, 0, :])[:, P * (i % 4):P * (i % 4 + 1)]
                last = pe.transpose(dst, xin[:, i, :], id_sb[:, :])
                if i % 4 == 3 or i == TT - 1:
                    last.then_inc(xT_raw, 1)
            pe.wait_ge(consts_in, CONSTS)
            pe.transpose(ps_o[:, 0:B1R], b1_rows[:, :], id_sb[0:B1R, 0:B1R]).then_inc(b1_raw, 1)
            pe.wait_ge(b1_done, 1)
            norm_tensor(pe, 0)

            def keys(b, j):
                pe.wait_ge(k_low, TH * b + j + 1)
                if isinstance(b, int) and b == 0:
                    if j > 0:
                        pe.wait_ge(kt_done, j)
                else:
                    pe.wait_ge(kt_done, TH * b + j)
                if j == 0 and (not isinstance(b, int) or b > 2):
                    pe.wait_ge(updated, b - 2)
                for half in range(2):
                    for c in range(CT):
                        cc = CT * j + c
                        last = pe.transpose(ps_kt[:, half, KE * c:KE * (c + 1)],
                                            k16[0:KE, half, D * cc:D * (cc + 1)], id16_sb[0:KE, 0:KE])
                last.then_inc(kt_raw, 1)

            def scores(b, u, n, t, j):
                if t == 0 and j == 0:
                    pe.wait_ge(q_ready, b + 1)
                    pe.wait_ge(kst_in, STACKED * (b + 1))
                if not isinstance(n, int) or n > 0:
                    pe.wait_ge(biased, TH * (n - 1) + j + 1)
                for g, r, m in pieces(t):
                    at = r - P * t
                    stack_ = kst[0:ST, u, KTE * (TH * g + j):KTE * (TH * g + j + 1)].rearrange("p (c k) -> p c k", k=KE)
                    last = pe.matmul(ps_s[at:at + m, j, 0:KT], qbd[0:ST, u, r:r + m], stack_[:, :, 0:KP],
                                     start=True, stop=True)
                last.then_inc(scored, 1)

            def transposes(n, s, q):
                if q == 0:
                    pe.wait_ge(probs, n + 1)
                if not isinstance(n, int) or n > 0:
                    if q < 2:
                        pe.wait_ge(t_act, 2 * (n - 1) + q + 1)
                    else:
                        pe.wait_ge(t_dve, n)
                for c in range(CT):
                    cc = CT * q + c
                    last = pe.transpose(ps_t[0:KP, q, P * c:P * (c + 1)], sc[:, s, KP * cc:KP * (cc + 1)], id_sb[:, :])
                last.then_inc(t_raw, 1)

            def attend(b, w, q):
                if q == 0:
                    pe.wait_ge(t_act, 2 * TILES * (b + 1))
                if q == TH - 1:
                    pe.wait_ge(t_dve, TILES * (b + 1))
                for c in range(CT * q, CT * (q + 1)):
                    for g in range(NG):
                        values = ring[w][0:KP, D * c + GD * g:D * c + GD * (g + 1)]
                        done = 0
                        if w % 2 == 1 and g == 0:
                            pe.matmul(ps_o[0:GD, 0:P], values, ptX[0:KP, P * c:P * (c + 1)], start=c == 0, stop=False)
                            done = P
                        last = pe.matmul(ps_o[GD * g:GD * (g + 1), done:GR], values,
                                         ptT[0:KP, ROWS * c + GR * g + done:ROWS * c + GR * (g + 1)],
                                         start=c == 0 and done == 0, stop=c == KC - 1)
                if q == TH - 1:
                    last.then_inc(values_used, 1)

            def spread_sums(b):
                pe.wait_ge(rsel_done, b + 1)
                for t in range(TILES):
                    for half in range(2):
                        last = pe.matmul(r_acc, rowhead_sb[:, t, :], rsel[:, half, t, :],
                                         start=t == 0 and half == 0, stop=t == TILES - 1 and half == 1)
                last.then_inc(attended, 1)

            def project(b):
                pe.wait_ge(combined, b + 1)
                if not isinstance(b, int) or b < B - 1:
                    pe.wait_ge(kt_done, TH * (b + 3) if not isinstance(b, int) or b < B - 2 else TH * B)
                pe.matmul(ps_m[:, 0:S], wout_sb[:, :], comb[:, :], start=True, stop=True).then_inc(projected, 1)

            for j in range(TH):
                keys(0, j)
            for j in range(TH):
                scores(0, 0, 0, 0, j)
            for j in range(2):
                keys(1, j)

            def batch(b, w, k, left, first=False):
                u = w % 2
                for t in range(TILES):
                    n = TILES * b + t
                    if t == 4 and not first:
                        project(b - 1)
                    for j in range(TH):
                        if t < TILES - 1:
                            scores(b, u, n + 1, t + 1, j)
                        elif left > 0:
                            scores(b + 1, 1 - u, n + 1, 0, j)
                        if not first and t == 2:
                            if j > 0:
                                attend(b - 1, (w - 1) % RING, j)
                        if not (first and t == 0):
                            transposes(n - 1, (u + t + 1) % 2, j)
                    if not first and t == 1:
                        attend(b - 1, (w - 1) % RING, 0)
                    if not first and t == 2:
                        spread_sums(b - 1)
                    if left > 0 and t == 0:
                        keys(b + 1, 2)
                    if left > 1 and t >= 5:
                        keys(b + 2, t - 5)
            batches(pe, batch)
            for j in range(TH):
                transposes(TILES * B - 1, (1 + TILES - 1) % 2, j)
            for j in range(TH):
                attend(B - 1, RING - 1, j)
            spread_sums(B - 1)
            project(B - 1)
            norm_tensor(pe, 1)
            mixture0_tensor(pe)
            norm_tensor(pe, 2)
            second_attention_tensor(pe)
            norm_tensor(pe, 3)
            mixture1_tensor(pe)


_INS = ["x", "ctx_1024", "fside_1x16xSxS2_0", "g_xattn", "g_ffn", "L0_xattn_w_out", "L0_ffn_router_w",
        "L0_ffn_router_b", "L0_ffn_W1", "L0_ffn_b1", "L0_ffn_W2", "L0_ffn_b2", "L1_xattn_scale_factor",
        "L1_ffn_W_router", "L1_ffn_b_router", "L1_ffn_W1", "L1_ffn_b1", "L1_ffn_W2", "L1_ffn_b2"]


def _constants():
    import numpy as np

    row = np.arange(ROWS).reshape(TILES, P).T
    part = np.arange(P)
    one = {
        "ident": np.eye(P, dtype=np.float32),
        "ident16": np.eye(P, dtype=np.float16),
        "diag4": (part[:, None] % GD // HD == np.arange(GH)).astype(np.float32),
        "diag4h": (part[:ST, None] % GD // HD == np.arange(GH)).astype(np.float16),
        "row_q": (row[:, :, None] % S == np.arange(S)).astype(np.float16),
        "row_head": (row[:, :, None] // S == part // HD).astype(np.float16),
        "sel0": (np.arange(E)[:, None, None] == 2 * np.arange(E // 2)[:, None] + part // F0).astype(np.float32),
        "sel1": np.broadcast_to(np.eye(E, dtype=np.float32)[:, :, None], (E, E, P)).copy(),
        "mean_w": np.full((P, P), 1.0 / D, np.float32),
        "centre_w": (np.eye(P) - 1.0 / D).astype(np.float32),
        "rank": np.broadcast_to(np.arange(E, 0, -1, dtype=np.float32), (P, E)).copy(),
    }
    return one


def kernel(**inputs):
    import numpy as _np
    import concourse.bacc as _bacc
    from concourse import mybir as _mybir
    from concourse.bass_utils import run_bass_kernel_spmd as _run

    nc = _bacc.Bacc("TRN2", target_bir_lowering=False, num_devices=1)
    arrays, args = {}, []
    for name in _INS:
        a = _np.ascontiguousarray(inputs[name])
        if a.ndim == 0:
            a = a.reshape(1)
        arrays[f"in_{name}_dram"] = a
        args.append(nc.dram_tensor(f"in_{name}_dram", a.shape, _mybir.dt.from_np(a.dtype), kind="ExternalInput").ap())
    for name, a in _constants().items():
        arrays[f"const_{name}_dram"] = a
        args.append(nc.dram_tensor(f"const_{name}_dram", a.shape, _mybir.dt.from_np(a.dtype), kind="ExternalInput").ap())
    args.append(nc.dram_tensor("out_dram", (B, S, D), _mybir.dt.float32, kind="ExternalOutput").ap())
    flamingo(nc, *args)
    r = _run(nc, [arrays], core_ids=[0])
    return r.results[0]["out_dram"]
```

```python
from contextlib import ExitStack

import concourse.bass as bass
from concourse import mybir

ACT = mybir.ActivationFunctionType
ALU = mybir.AluOpType
AX = mybir.AxisListType
F32 = mybir.dt.float32
F16 = mybir.dt.float16

P = 128
B, S, D, S2 = 32, 56, 128, 1500
H = 16
HD = D // H
T = B * S
ROWS = H * S
TILES = ROWS // P
KP = 125
KC = S2 // KP
TH = 3
KT = S2 // TH
CT = KC // TH
KE = KP + 1
KTE = CT * KE
GH = 4
NG = H // GH
GR = GH * S
GD = GH * HD
TERMS = 3
STACKED = 16 * TERMS * NG
ST = TERMS * GD
TT = T // P
NQ = 4
TQ = T // NQ
E = 8
F0, F1 = 64, 512
EPS = 1e-5
PRODUCTS = ((0, 0), (1, 0), (0, 1))
BANK = 512
RING = 4
HALF = 64
SCALE0 = HD ** -0.5
ROUTE_EXP = 13
ROUTE_STEPS = 18


def pieces(t):
    out, r = [], t * P
    while r < (t + 1) * P:
        g = r // GR
        n = min((g + 1) * GR, (t + 1) * P) - r
        at = r - t * P
        if n < P:
            n = 64 if n >= 64 and at % 64 == 0 else 32
        out.append((g, r, n))
        r += n
    return out


def flamingo(nc, x, ctx_, bias, g_xattn, g_ffn, w_out, r_w0, r_b0, w1_0, b1_0, w2_0, b2_0, scale1,
             r_w1, r_b1, w1_1, b1_1, w2_1, b2_1, ident, ident16, diag4, diag4h, row_q, row_head,
             sel0, sel1, mean_w, centre_w, rank, out):
    with ExitStack() as stack:
        def sb(name, shape, dt=F32):
            return stack.enter_context(nc.sbuf_tensor(name, shape, dt))

        def sem(name):
            return stack.enter_context(nc.semaphore(name))

        resid = sb("resid", [P, T])
        normed = sb("normed", [P, T])
        bias_sb = sb("bias_sb", [P, TILES, S2])
        ptT = sb("ptT", [P, KC * ROWS])
        sc = sb("sc", [P, 2, S2])
        kv = sb("kv", [P, 2, KC * D])
        kvx = sb("kvx", [P, KC * D])
        ring = [kv[:, 0, :], kv[:, 1, :], kvx[:, :], normed[:, 0:KC * D]]
        k16 = sb("k16", [P, 2, KC * D], F16)
        kT16 = sb("kT16", [P, 2, KC * KE], F16)
        kst = sb("kst", [P, 2, NG * KC * KE], F16)
        qst = sb("qst", [P, NG, T], F16)
        qbd = sb("qbd", [P, 2, ROWS], F16)
        mx = sb("mx", [P, 2, TH])
        negmax = sb("negmax", [P, 2])
        rowsum = sb("rowsum", [P, 2, TILES])
        rs16 = sb("rs16", [P, 2, TILES], F16)
        rsel = sb("rsel", [P, 2, TILES, S], F16)
        o_mask = sb("o_mask", [P, GH, S])
        o_sum = sb("o_sum", [P, S])
        r_inv = sb("r_inv", [P, S])
        comb = sb("comb", [P, S])
        wout_sb = sb("wout_sb", [P, D])
        id_sb = sb("id_sb", [P, P])
        id16_sb = sb("id16_sb", [P, P], F16)
        diag4_sb = sb("diag4_sb", [P, GH])
        diag4h_sb = sb("diag4h_sb", [P, GH], F16)
        rowq_sb = sb("rowq_sb", [P, TILES, S], F16)
        rowhead_sb = sb("rowhead_sb", [P, TILES, P], F16)
        mean_sb = sb("mean_sb", [P, P])
        centre_sb = sb("centre_sb", [P, P])
        std = sb("std", [P, 2, TT])
        rank_sb = sb("rank_sb", [P, E])
        gates_in = sb("gates_in", [P, 4])
        gates = sb("gates", [P, 4])
        scale_sb = sb("scale_sb", [P, 1])
        eps_sb = sb("eps_sb", [P, 1])
        rw_sb = sb("rw_sb", [P, 2, E])
        rb_sb = sb("rb_sb", [P, 2, E])
        w10_sb = sb("w10_sb", [P, E, F0])
        w20_sb = sb("w20_sb", [P, E // 2, D])
        B1R = E // 2 + E * F1 // P
        b1_rows = sb("b1_rows", [B1R, P])
        b1T = sb("b1T", [P, B1R])
        b10_sb = b1T[:, 0:E // 2]
        b11_sb = b1T[:, E // 2:B1R].rearrange("p (e k) -> p e k", e=E)
        b2_sb = sb("b2_sb", [E, 2, D])
        bias_flat = bias_sb[:, :, :].rearrange("p a n -> p (a n)")
        w11_sb = bias_flat[:, 0:E * F1].rearrange("p (e f) -> p e f", e=E)
        w21_sb = bias_flat[:, E * F1:2 * E * F1].rearrange("p (e k d) -> p e k d", e=E, k=F1 // P)
        WH = E * F1 // 2
        LATE = 4 * S2 + KC * P
        w1_parts = [ptT[:, LATE:LATE + WH], bias_flat[:, 2 * E * F1:2 * E * F1 + WH]]
        w2_parts = [bias_flat[:, 0:WH], bias_flat[:, WH:2 * WH]]
        w1_halves = [a.bitcast(F16).rearrange("p (e f) -> p e f", e=E) for a in w1_parts]
        w2_halves = [a.bitcast(F16).rearrange("p (e k d) -> p e k d", e=E, k=F1 // P) for a in w2_parts]
        XT = 2
        ptX = sb("ptX", [P, KC * XT * P])
        sel0_sb = ptX[0:E, 0:P * (E // 2)].rearrange("e (i p) -> e i p", p=P)
        sel1_sb = ptX[0:E, P * (E // 2):P * E].bitcast(F16).rearrange("e (i p) -> e i p", p=P)
        qbd_f = qbd[:, :, :].rearrange("p a n -> p (a n)").bitcast(F32)
        rt = [qbd_f[:, TT * E * i:TT * E * (i + 1)].rearrange("p (i e) -> p i e", e=E) for i in range(4)]
        rm = sb("rm", [P, 4, TT])
        wT = sc[:, :, :].rearrange("p a n -> p (a n)")[0:E, 0:T]
        sq = ptT[:, 0:T]
        h16 = ptT[:, 2 * T:3 * T].bitcast(F16)[:, 0:T]
        l16 = ptT[:, 3 * T:4 * T].bitcast(F16)[:, 0:T]
        diag = ptT[:, T:2 * T]
        mix = ptT[:, 2 * T:2 * T + 4 * TQ].rearrange("p (s n) -> p s n", n=TQ)
        k2T = ptT[:, 0:4 * S2].rearrange("p (r u n) -> p r u n", r=2, u=2)
        p2T = ptT[:, 4 * S2:4 * S2 + KC * P].rearrange("p (c n) -> p c n", n=P)
        kst_f = kst[:, :, :].rearrange("p a n -> p (a n)").bitcast(F32)
        qst_f = qst[:, :, :].rearrange("p a n -> p (a n)").bitcast(F32)
        kst_parts = [kst_f[:, KC * D * i:KC * D * (i + 1)] for i in range(3)]
        kv2 = [[kv[:, 0, :], kv[:, 1, :]], kst_parts[0:2], [kst_parts[2], kvx[:, :]],
               [qst_f[:, 0:KC * D], qst_f[:, KC * D:2 * KC * D]]]
        FK = F1 // P
        halves = kst_f[:, 0:2 * 2 * FK * TQ // 2].bitcast(F16).rearrange("p (r h f n) -> p r h f n", r=2, h=2, f=FK)
        whole = kst_f[:, 2 * FK * TQ:3 * FK * TQ].rearrange("p (f n) -> p f n", f=FK)
        work = qst_f[:, 0:4 * TQ].rearrange("p (s n) -> p s n", n=TQ)
        x_halves = qst_f[:, 4 * TQ:4 * TQ + T].bitcast(F16).rearrange("p (h n) -> p h n", h=2)
        w_halves = kv[0:E, :, :].rearrange("p a n -> p (a n)")[:, 0:T].bitcast(F16).rearrange("p (h n) -> p h n", h=2)
        q2 = qbd_f[:, 4 * TT * E:4 * TT * E + 4 * HALF].rearrange("p (r u n) -> p r u n", r=2, u=2)
        o2 = sb("o2", [P, D])
        r2 = sb("r2", [P, 1])
        xin = sc[:, :, :].rearrange("p a n -> p (a n)")[:, 0:T].rearrange("p (i d) -> p i d", d=D)

        ps_s = stack.enter_context(nc.psum_tensor("ps_s", [P, TH, BANK], F32))
        ps_t = stack.enter_context(nc.psum_tensor("ps_t", [P, TH, BANK], F32))
        ps_o = stack.enter_context(nc.psum_tensor("ps_o", [P, BANK], F32))
        ps_m = stack.enter_context(nc.psum_tensor("ps_m", [P, BANK], F32))
        ps_kt = ps_m[:, :].bitcast(F16).rearrange("p (a n) -> p a n", a=2)
        pv_acc = ps_o[:, 0:GR]
        r_acc = ps_o[:, 256:256 + S]

        passed = sem("passed")
        ident_in = sem("ident_in")
        early_in = sem("early_in")
        consts_in = sem("consts_in")
        x_in = sem("x_in")
        bias_in = sem("bias_in")
        xT_raw = sem("xT_raw")
        xT_done = sem("xT_done")
        b1_raw = sem("b1_raw")
        b1_done = sem("b1_done")
        eps_set = sem("eps_set")
        gates_done = sem("gates_done")
        ln_cent = sem("ln_cent")
        ln_sq = sem("ln_sq")
        ln_out = sem("ln_out")
        ln_var = sem("ln_var")
        ln_std = sem("ln_std")
        ln_inv = sem("ln_inv")
        ln_diag = sem("ln_diag")
        ln_spread = sem("ln_spread")
        ln_done = sem("ln_done")
        q_high = sem("q_high")
        q_low = sem("q_low")
        qst_in = sem("qst_in")
        keys_in = [sem(f"keys_in{w}") for w in range(RING)]
        late_in = sem("late_in")
        k_zero = sem("k_zero")
        k_high = sem("k_high")
        k_low = sem("k_low")
        kt_raw = sem("kt_raw")
        kt_done = sem("kt_done")
        kst_in = sem("kst_in")
        q_ready = sem("q_ready")
        scored = sem("scored")
        biased = sem("biased")
        negmaxed = sem("negmaxed")
        probs = sem("probs")
        t_raw = sem("t_raw")
        t_act = sem("t_act")
        t_dve = sem("t_dve")
        rs_part = sem("rs_part")
        rsel_done = sem("rsel_done")
        values_used = sem("values_used")
        attended = sem("attended")
        comb_step = sem("comb_step")
        combined = sem("combined")
        projected = sem("projected")
        updated = sem("updated")
        logits = sem("logits")
        route_step = sem("route_step")
        route_exp = sem("route_exp")
        routed = sem("routed")
        wT_raw = sem("wT_raw")
        wT_done = sem("wT_done")
        hidden0 = sem("hidden0")
        spread0 = sem("spread0")
        gelu_done = sem("gelu_done")
        weighted = sem("weighted")
        y_part = sem("y_part")
        mixed0 = sem("mixed0")
        w1_in = sem("w1_in")
        hidden1 = sem("hidden1")
        hid_high = sem("hid_high")
        hid_low = sem("hid_low")
        w_split = sem("w_split")
        x_high = sem("x_high")
        x_low = sem("x_low")
        w_high = sem("w_high")
        w_low = sem("w_low")
        spread1 = sem("spread1")
        spread_out = sem("spread_out")
        b2_sum = sem("b2_sum")
        acc_set = sem("acc_set")
        y_done = sem("y_done")
        y_mul = sem("y_mul")
        y_add = sem("y_add")
        mixed1 = sem("mixed1")
        ctx2_in = [[sem(f"ctx2_in{w}{u}") for u in range(2)] for w in range(RING)]
        q2_zero = sem("q2_zero")
        q2_done = sem("q2_done")
        t2_raw = sem("t2_raw")
        e2_act = sem("e2_act")
        e2_dve = sem("e2_dve")
        scored2 = sem("scored2")
        negmax2 = sem("negmax2")
        probs2 = sem("probs2")
        pv2 = sem("pv2")
        inv2 = sem("inv2")
        normal2 = sem("normal2")
        o2_raw = sem("o2_raw")
        updated2 = sem("updated2")
        out_raw = sem("out_raw")
        out_sb = sem("out_sb")
        stored = sem("stored")

        early = [(centre_sb[:, :], centre_w), (id16_sb[:, :], ident16), (mean_sb[:, :], mean_w)]
        consts = [
            (diag4_sb[:, :], diag4), (diag4h_sb[0:ST, :], diag4h), (rowq_sb[:, :, :], row_q),
            (rowhead_sb[:, :, :], row_head), (wout_sb[:, :], w_out),
            (gates_in[:, 0:2], g_xattn.partition_broadcast(P)), (gates_in[:, 2:4], g_ffn.partition_broadcast(P)),
            (scale_sb[:, :], scale1.partition_broadcast(P)),
            (rank_sb[:, :], rank),
            (rw_sb[:, 0, :], r_w0), (rw_sb[:, 1, :], r_w1),
            (rb_sb[:, 0, :], r_b0.partition_broadcast(P)), (rb_sb[:, 1, :], r_b1.partition_broadcast(P)),
            (w10_sb[:, :, :], w1_0.rearrange("e d f -> d e f")),
            (w20_sb[:, :, :], w2_0.rearrange("(i e) f d -> (e f) i d", e=2)),
            (b1_rows[0:E // 2, :], b1_0.rearrange("(i e) f -> i (e f)", e=2)),
            (b1_rows[E // 2:B1R, :], b1_1.rearrange("e (k p) -> (e k) p", p=P)),
            (b2_sb[:, 0, :], b2_0), (b2_sb[:, 1, :], b2_1),
        ]
        CONSTS = 16 * len(consts)
        ctx_v = ctx_.rearrange("b (c p) d -> b p c d", p=KP)
        bias_v = bias.rearrange("a h q k -> (a h q) k").rearrange("(t p) k -> p t k", p=P)

        def third(j):
            return slice(CT * D * j, CT * D * (j + 1))

        def transposed(u, t, q):
            if u == 1 and t < XT:
                return ptX[0:KP, :].rearrange("p (c r) -> p c r", r=XT * P)[:, CT * q:CT * (q + 1), P * t:P * (t + 1)]
            return ptT[0:KP, :].rearrange("p (c r) -> p c r", r=ROWS)[:, CT * q:CT * (q + 1), P * t:P * (t + 1)]

        def rounds(eng, body, n):
            body(0, 0, 0, 2, first=True)
            with eng.Fori(0, n // RING - 1) as i:
                for d in range(1, RING + 1):
                    body(RING * i + d, d % RING, i + d // RING, 2)
            for left in (2, 1, 0):
                body(n - 1 - left, RING - 1 - left, n // RING - 1, left)

        def ahead(b, w, k, d):
            return b + d, (w + d) % RING, k + (w + d) // RING

        NORM_IN = [(xT_done, NQ), (updated, B), (mixed0, NQ), (updated2, B // 2)]

        def chunk(c):
            return slice(TQ * c, TQ * (c + 1))

        def norm_cols(c):
            return slice(BANK * c, min(BANK * (c + 1), T))

        def centred(c):
            bank = ps_s[:, c, :] if c < TH else ps_t[:, 0, :]
            return bank[:, 0:min(BANK, T - BANK * c)]

        def spread_std(c):
            return (ps_t[:, 1, :], ps_t[:, 2, :], ps_o[:, :], ps_m[:, :])[c][:, 0:min(BANK, T - BANK * c)]

        variances = ps_m[:, BANK - TT:BANK]

        def centre_tensor(pe, r):
            sem_in, n_in = NORM_IN[r]
            pe.wait_ge(sem_in, n_in)
            for c in range(NQ):
                pe.matmul(centred(c), centre_sb[:, :], resid[:, norm_cols(c)], start=True, stop=True).then_inc(ln_cent, 1)

        def norm_tensor(pe, r):
            if r > 0:
                centre_tensor(pe, r)
            for i in range(TT):
                if i % 4 == 0:
                    pe.wait_ge(ln_sq, NQ * r + i // 4 + 1)
                last = pe.matmul(variances[:, i:i + 1], sq[:, P * i:P * (i + 1)], mean_sb[:, 0:1], start=True, stop=True)
            last.then_inc(ln_var, 1)
            for c in range(NQ):
                pe.wait_ge(ln_diag, TT * r + min(4 * (c + 1), TT))
                pe.matmul(spread_std(c), mean_sb[:, :], diag[:, norm_cols(c)], start=True, stop=True).then_inc(ln_spread, 1)

        def norm_scalar(act, r):
            for c in range(NQ):
                act.wait_ge(ln_out, NQ * r + c + 1)
                act.activation(sq[:, norm_cols(c)], normed[:, norm_cols(c)], ACT.Square).then_inc(ln_sq, 1)
            act.wait_ge(eps_set, 1)
            act.wait_ge(ln_var, r + 1)
            act.activation(std[:, 0, :], variances, ACT.Sqrt, bias=eps_sb[:, 0:1], scale=1.0 / D ** 2).then_inc(ln_std, 1)

        def norm_vector(dve, r):
            for c in range(NQ):
                dve.wait_ge(ln_cent, NQ * r + c + 1)
                dve.tensor_copy(normed[:, norm_cols(c)], centred(c)).then_inc(ln_out, 1)
            dve.wait_ge(ln_std, r + 1)
            dve.reciprocal(std[:, 1, :], std[:, 0, :]).then_inc(ln_inv, 1)
            dve.wait_ge(ln_inv, r + 1)
            for i in range(TT):
                dve.tensor_scalar(diag[:, P * i:P * (i + 1)], id_sb[:, :], std[:, 1, i:i + 1], None, ALU.mult).then_inc(ln_diag, 1)
            for c in range(NQ):
                dve.wait_ge(ln_out, NQ * r + c + 1)
                dve.wait_ge(ln_spread, NQ * r + c + 1)
                dve.tensor_tensor(normed[:, norm_cols(c)], normed[:, norm_cols(c)], spread_std(c), ALU.mult).then_inc(ln_done, 1)

        def four_tiles(i):
            bank = ps_s[:, i // 4, :] if i < 4 * TH else ps_t[:, 0, :]
            return bank[:, P * (i % 4):P * (i % 4 + 1)]

        def route_tensor(pe, layer):
            pe.wait_ge(ln_done, NQ * (2 * layer + 2))
            for i in range(TT):
                last = pe.matmul(ps_o[:, E * i:E * (i + 1)], normed[:, P * i:P * (i + 1)], rw_sb[:, layer, :], start=True, stop=True)
            last.then_inc(logits, 1)
            pe.wait_ge(routed, layer + 1)
            for i in range(TT):
                last = pe.transpose(four_tiles(i)[0:E, :], rt[2][:, i, :], id_sb[:, :])
            last.then_inc(wT_raw, 1)

        def route_scalar(act, layer):
            act.wait_ge(route_step, ROUTE_STEPS * layer + ROUTE_EXP)
            act.activation(rm[:, 3, :], rm[:, 2, :], ACT.Exp).then_inc(route_exp, 1)

        def route_vector(dve, layer):
            step = [ROUTE_STEPS * layer]

            def link(instruction):
                step[0] += 1
                instruction.then_inc(route_step, 1)
                dve.wait_ge(route_step, step[0])

            def per_token(v):
                return v.unsqueeze(2).broadcast_to([P, TT, E])

            def one_hot(dst, src, top):
                link(dve.tensor_reduce(rm[:, top, :], src[:, :, :], axis=AX.X, op=ALU.max))
                link(dve.tensor_tensor(dst[:, :, :], src[:, :, :], per_token(rm[:, top, :]), ALU.is_equal))
                link(dve.tensor_tensor(dst[:, :, :], dst[:, :, :], rank_sb[:, :].unsqueeze(1).broadcast_to([P, TT, E]), ALU.mult))
                link(dve.tensor_reduce(rm[:, 1, :], dst[:, :, :], axis=AX.X, op=ALU.max))
                link(dve.tensor_tensor(dst[:, :, :], dst[:, :, :], per_token(rm[:, 1, :]), ALU.is_equal))

            dve.wait_ge(logits, layer + 1)
            link(dve.tensor_tensor(rt[0][:, :, :], ps_o[:, 0:TT * E].rearrange("p (i e) -> p i e", e=E),
                                   rb_sb[:, layer, :].unsqueeze(1).broadcast_to([P, TT, E]), ALU.add))
            one_hot(rt[1], rt[0], 0)
            link(dve.scalar_tensor_tensor(out=rt[2][:, :, :], in0=rt[1][:, :, :], scalar=-3.0e38, in1=rt[0][:, :, :],
                                          op0=ALU.mult, op1=ALU.add))
            one_hot(rt[3], rt[2], 2)
            link(dve.tensor_tensor(rm[:, 2, :], rm[:, 2, :], rm[:, 0, :], ALU.subtract))
            assert step[0] == ROUTE_STEPS * layer + ROUTE_EXP
            dve.wait_ge(route_exp, layer + 1)
            link(dve.tensor_scalar(rm[:, 0, :], rm[:, 3, :], 1.0, None, ALU.add))
            link(dve.reciprocal(rm[:, 1, :], rm[:, 0, :]))
            link(dve.tensor_tensor(rm[:, 2, :], rm[:, 3, :], rm[:, 1, :], ALU.mult))
            link(dve.tensor_tensor(rt[1][:, :, :], rt[1][:, :, :], per_token(rm[:, 1, :]), ALU.mult))
            link(dve.tensor_tensor(rt[3][:, :, :], rt[3][:, :, :], per_token(rm[:, 2, :]), ALU.mult))
            assert step[0] == ROUTE_STEPS * (layer + 1)
            dve.tensor_tensor(rt[2][:, :, :], rt[1][:, :, :], rt[3][:, :, :], ALU.add).then_inc(routed, 1)
            dve.wait_ge(wT_raw, layer + 1)
            for c in range(NQ):
                n = min(4 * P, T - 4 * P * c)
                bank = ps_s[:, c, :] if c < TH else ps_t[:, 0, :]
                dve.tensor_copy(wT[:, 4 * P * c:4 * P * c + n], bank[0:E, 0:n]).then_inc(wT_done, 1)

        PAIRS = E // 2

        def y0_bank(c):
            return (ps_o if c % 2 else ps_m)[:, 0:TQ]

        def mixture0_tensor(pe):
            route_tensor(pe, 0)
            pe.wait_ge(late_in, 32)
            pe.wait_ge(wT_done, NQ)

            def output(k):
                c, i = divmod(k, PAIRS)
                if i == 0:
                    if c >= 2:
                        pe.wait_ge(mixed0, c - 1)
                    pe.matmul(y0_bank(c), b2_sb[:, 0, :], wT[:, chunk(c)], start=True, stop=False)
                pe.wait_ge(weighted, k + 1)
                pe.matmul(y0_bank(c), w20_sb[:, i, :], mix[:, 2 + k % 2, :], start=False, stop=i == PAIRS - 1).then_inc(y_part, 1)

            for k in range(NQ * PAIRS):
                c, i = divmod(k, PAIRS)
                if k >= 2:
                    pe.wait_ge(gelu_done, k - 1)
                pe.matmul(ps_s[:, k % 2, 0:TQ], w10_sb[:, 2 * i:2 * i + 2, :].rearrange("p e f -> p (e f)"),
                          normed[:, chunk(c)], start=True, stop=True).then_inc(hidden0, 1)
                if k >= 2:
                    pe.wait_ge(weighted, k - 1)
                pe.matmul(ps_t[:, k % 2, 0:TQ], sel0_sb[:, i, :], wT[:, chunk(c)], start=True, stop=True).then_inc(spread0, 1)
                if k >= 1:
                    output(k - 1)
            output(NQ * PAIRS - 1)

        def mixture0_scalar(act):
            route_scalar(act, 0)
            for k in range(NQ * PAIRS):
                act.wait_ge(hidden0, k + 1)
                if k >= 2:
                    act.wait_ge(weighted, k - 1)
                act.activation(mix[:, k % 2, :], ps_s[:, k % 2, 0:TQ], ACT.Gelu, bias=b10_sb[:, k % PAIRS:k % PAIRS + 1]).then_inc(gelu_done, 1)

        def mixture0_vector(dve):
            route_vector(dve, 0)
            for k in range(NQ * PAIRS):
                c, i = divmod(k, PAIRS)
                dve.wait_ge(gelu_done, k + 1)
                dve.wait_ge(spread0, k + 1)
                if k >= 2:
                    dve.wait_ge(y_part, k - 1)
                dve.tensor_tensor(mix[:, 2 + k % 2, :], mix[:, k % 2, :], ps_t[:, k % 2, 0:TQ], ALU.mult).then_inc(weighted, 1)
                if i == PAIRS - 1:
                    dve.wait_ge(y_part, k + 1)
                    dve.scalar_tensor_tensor(out=resid[:, chunk(c)], in0=y0_bank(c), scalar=gates[:, 2:3], in1=resid[:, chunk(c)],
                                             op0=ALU.mult, op1=ALU.add).then_inc(mixed0, 1)

        NP2 = B // 2
        T2, A2, V2 = 3 * TH, 3 * (TH - 1), 3

        def turned_before(p, left):
            return T2 * p + 4 * TH - (2 * TH if left == 0 else 0)

        def act_before(p, left):
            return A2 * p + 4 * (TH - 1) - (2 * (TH - 1) if left == 0 else 0)

        def dve_before(p, left):
            return V2 * p + 4 - (2 if left == 0 else 0)

        def second_attention_sync(sp):
            def load(p, w):
                for u in range(2):
                    sp.dma_start(kv2[w][u][0:KP, :].rearrange("p (c d) -> p c d", d=D),
                                 ctx_v[bass.ds(2 * p + u, 1), :, :, :].rearrange("a p c d -> p (a c) d")).then_inc(ctx2_in[w][u], 16)

            sp.wait_ge(attended, B)
            for dst, src in ((sel0_sb, sel0), (sel1_sb, sel1)):
                sp.dma_start(dst, src).then_inc(late_in, 16)
            load(0, 0)
            for dst, src in ((w11_sb, w1_1.rearrange("e d f -> d e f")),
                             (w21_sb, w2_1.rearrange("e (k p) d -> p e k d", p=P))):
                sp.dma_start(dst, src).then_inc(w1_in, 16)
            for p in range(1, RING):
                load(p, p)
            with sp.Fori(0, NP2 // RING - 1) as i:
                for d in range(1, RING + 1):
                    p = RING * i + d
                    sp.wait_ge(pv2, p)
                    sp.sem_inc(passed, 1)
                    load(p + RING - 1, (d - 1) % RING)
            for c in range(NQ):
                n = min(4, TT - 4 * c)
                sp.wait_ge(out_sb, c + 1)
                sp.dma_start(out.rearrange("b s d -> (b s) d")[4 * P * c:4 * P * c + P * n, :].rearrange("(i p) d -> p i d", p=P),
                             xin[:, 4 * c:4 * c + n, :]).then_inc(stored, 16)
            sp.wait_ge(stored, 16 * NQ)

        def split_weights(pool):
            pool.wait_ge(w1_in, 32)
            flat = (bias_flat[:, 0:E * F1], bias_flat[:, E * F1:2 * E * F1])
            for i, (src, parts) in enumerate(zip(flat, (w1_parts, w2_parts))):
                high, low = (part.bitcast(F16) for part in parts)
                pool.tensor_copy(high, src).then_inc(w_split, 1)
                pool.wait_ge(w_split, 2 * i + 1)
                pool.tensor_tensor(low, src, high, ALU.subtract).then_inc(w_split, 1)
                pool.wait_ge(w_split, 2 * i + 2)

        def second_attention_pool(pool):
            pool.wait_ge(ln_done, NQ * 3)
            pool.memset(q2[:, :, :, :], 0.0).then_inc(q2_zero, 1)
            pool.wait_ge(q2_zero, 1)

            def queries(p, r):
                pool.tensor_tensor(q2[:, r, :, 0:S], normed[:, bass.ds(2 * S * p, 2 * S)].rearrange("p (u q) -> p u q", u=2),
                                   scale_sb[:, 0:1].unsqueeze(2).broadcast_to([P, 2, S]), ALU.mult).then_inc(q2_done, 1)

            queries(0, 0)
            queries(1, 1)

            def pair(p, w, k, left, first=False):
                if left > 1:
                    pool.wait_ge(scored2, p + 1)
                    queries(p + 2, w % 2)

            rounds(pool, pair, NP2)

        def second_attention_scalar(act):
            def key_out(r, u, count):
                for j in range(TH - 1):
                    act.wait_ge(t2_raw, count + j + 1)
                    act.activation(k2T[:, r, u, KT * j:KT * (j + 1)], ps_t[:, j, 0:KT], ACT.Copy).then_inc(e2_act, 1)

            def exponent(p, r):
                act.wait_ge(negmax2, p + 1)
                act.activation(sc[:, r, :].rearrange("p (j n) -> p j n", j=TH), ps_s[:, :, 0:KT], ACT.Exp, bias=negmax[:, 0:1],
                               accum_out=rowsum[:, r, 0:1]).then_inc(probs2, 1)

            act.wait_ge(ln_done, NQ * 3)
            for u in range(2):
                key_out(0, u, TH * u)
            exponent(0, 0)
            for u in range(2):
                key_out(1, u, TH * (2 + u))

            def pair(p, w, k, left, first=False):
                before = turned_before(p, left)
                for q in range(TH - 1):
                    act.wait_ge(t2_raw, before + q + 1)
                    act.activation(p2T[0:KP, CT * q:CT * (q + 1), :], ps_t[0:KP, q, :].rearrange("p (c n) -> p c n", n=P),
                                   ACT.Copy).then_inc(e2_act, 1)
                if left > 1:
                    key_out(w % 2, 0, before + TH)
                if left > 0:
                    exponent(p + 1, (w + 1) % 2)
                if left > 1:
                    key_out(w % 2, 1, before + 2 * TH)

            rounds(act, pair, NP2)

        def second_attention_vector(dve):
            def key_out(r, u, count):
                dve.wait_ge(t2_raw, count + TH)
                dve.tensor_copy(k2T[:, r, u, 2 * KT:3 * KT], ps_t[:, 2, 0:KT]).then_inc(e2_dve, 1)

            def maximum(p):
                dve.wait_ge(scored2, p + 1)
                dve.tensor_reduce(negmax[:, 0:1], ps_s[:, :, 0:KT], axis=AX.XY, op=ALU.max, negate=True).then_inc(negmax2, 1)

            def update(p):
                dve.wait_ge(o2_raw, p + 1)
                r = resid[:, bass.ds(2 * S * p, 2 * S)].rearrange("p (u q) -> p u q", u=2)
                dve.scalar_tensor_tensor(out=r, in0=ps_m[:, 0:P].rearrange("p (u q) -> p u q", u=2)[:, :, 0:S],
                                         scalar=gates[:, 1:2], in1=r, op0=ALU.mult, op1=ALU.add).then_inc(updated2, 1)

            for u in range(2):
                key_out(0, u, TH * u)
            maximum(0)
            for u in range(2):
                key_out(1, u, TH * (2 + u))

            def pair(p, w, k, left, first=False):
                before = turned_before(p, left)
                if left > 0:
                    maximum(p + 1)
                dve.wait_ge(t2_raw, before + TH)
                dve.tensor_copy(p2T[0:KP, 2 * CT:3 * CT, :], ps_t[0:KP, 2, :].rearrange("p (c n) -> p c n", n=P)).then_inc(e2_dve, 1)
                if not first:
                    update(p - 1)
                if left > 1:
                    key_out(w % 2, 0, before + TH)
                    key_out(w % 2, 1, before + 2 * TH)
                dve.wait_ge(probs2, p + 1)
                dve.reciprocal(r2[:, 0:1], rowsum[:, w % 2, 0:1]).then_inc(inv2, 1)
                dve.wait_ge(inv2, p + 1)
                dve.wait_ge(pv2, p + 1)
                dve.tensor_scalar(o2[:, :], ps_o[:, 0:D], r2[:, 0:1], None, ALU.mult).then_inc(normal2, 1)

            rounds(dve, pair, NP2)
            update(NP2 - 1)

        def second_attention_tensor(pe):
            def bank_free(j, act_count, dve_count):
                if j < TH - 1:
                    pe.wait_ge(e2_act, act_count - (TH - 1) + j + 1)
                else:
                    pe.wait_ge(e2_dve, dve_count)

            def turn_keys(w, k, u, act_count, dve_count):
                pe.wait_ge(ctx2_in[w][u], 16 * (k + 1))
                for j in range(TH):
                    if not isinstance(act_count, int) or act_count > 0:
                        bank_free(j, act_count, dve_count)
                    for c in range(CT):
                        cc = CT * j + c
                        last = pe.transpose(ps_t[:, j, KP * c:KP * (c + 1)], kv2[w][u][0:KP, D * cc:D * (cc + 1)], id_sb[0:KP, 0:KP])
                    last.then_inc(t2_raw, 1)

            def scores(p, r, act_count, dve_count):
                pe.wait_ge(q2_done, p + 1)
                pe.wait_ge(e2_act, act_count)
                pe.wait_ge(e2_dve, dve_count)
                if not isinstance(p, int) or p > 0:
                    pe.wait_ge(probs2, p)
                for j in range(TH):
                    for u in range(2):
                        last = pe.matmul(ps_s[HALF * u:HALF * (u + 1), j, 0:KT], q2[:, r, u, :], k2T[:, r, u, KT * j:KT * (j + 1)],
                                         start=True, stop=True)
                last.then_inc(scored2, 1)

            def turn_output(p):
                pe.wait_ge(normal2, p + 1)
                pe.transpose(ps_m[:, 0:P], o2[:, :], id_sb[:, :]).then_inc(o2_raw, 1)

            pe.wait_ge(ln_done, NQ * 3)
            for u in range(2):
                turn_keys(0, 0, u, (TH - 1) * u, u)
            scores(0, 0, 2 * (TH - 1), 2)
            for u in range(2):
                turn_keys(1, 0, u, (TH - 1) * (2 + u), 2 + u)

            def pair(p, w, k, left, first=False):
                acts, dves = act_before(p, left), dve_before(p, left)
                if left > 0:
                    scores(p + 1, (w + 1) % 2, acts, dves)
                pe.wait_ge(probs2, p + 1)
                for q in range(TH):
                    bank_free(q, acts, dves)
                    for c in range(CT):
                        cc = CT * q + c
                        last = pe.transpose(ps_t[0:KP, q, P * c:P * (c + 1)], sc[:, w % 2, KP * cc:KP * (cc + 1)], id_sb[:, :])
                    last.then_inc(t2_raw, 1)
                if not first:
                    turn_output(p - 1)
                _, w2, k2 = ahead(p, w, k, 2)
                if left > 1:
                    turn_keys(w2, k2, 0, acts + (TH - 1), dves + 1)
                for c in range(KC):
                    if c == 2 * CT and left > 1:
                        turn_keys(w2, k2, 1, acts + 2 * (TH - 1), dves + 2)
                    if c % CT == 0:
                        q = c // CT
                        if q < TH - 1:
                            pe.wait_ge(e2_act, acts + q + 1)
                        else:
                            pe.wait_ge(e2_dve, dves + 1)
                    for u in range(2):
                        last = pe.matmul(ps_o[HALF * u:HALF * (u + 1), 0:D], p2T[0:KP, c, HALF * u:HALF * (u + 1)],
                                         kv2[w][u][0:KP, D * c:D * (c + 1)], start=c == 0, stop=c == KC - 1)
                last.then_inc(pv2, 1)

            rounds(pe, pair, NP2)
            turn_output(NP2 - 1)

        def chunks(eng, body):
            body(0, first=True)
            with eng.Fori(1, NQ) as c:
                body(c)

        def tokens(c):
            return bass.ds(TQ * c, TQ)

        def hidden_bank(f):
            return (ps_s[:, f, 0:TQ] if f < TH else ps_t[:, 0, 0:TQ])

        def y1_bank(e):
            return (ps_o if e % 2 else ps_m)[:, 0:TQ]

        def mixture1_tensor(pe):
            route_tensor(pe, 1)
            pe.wait_ge(wT_done, 2 * NQ)
            pe.wait_ge(w_split, 4)
            pe.wait_ge(x_low, NQ)

            def output(k, e, f):
                if f == 0 and (not isinstance(k, int) or k >= 2):
                    pe.wait_ge(y_mul, k - 1)
                pe.wait_ge(hid_low, FK * k + f + 1)
                for i, (wh, hh) in enumerate(PRODUCTS):
                    last = pe.matmul(y1_bank(e), w2_halves[wh][:, e, f, :], halves[:, e % 2, hh, f, :],
                                     start=f == 0 and i == 0, stop=f == FK - 1 and i == 2)
                if f == FK - 1:
                    last.then_inc(y_done, 1)

            def body(c, first=False):
                for e in range(E):
                    k = E * c + e
                    start = first and e == 0
                    for f in range(FK):
                        if not start:
                            pe.wait_ge(hid_high, FK * (k - 1) + f + 1)
                            pe.sem_inc(passed, 1)
                        for i, (wh, xh) in enumerate(PRODUCTS):
                            last = pe.matmul(hidden_bank(f), w1_halves[wh][:, e, P * f:P * (f + 1)], x_halves[:, xh, tokens(c)],
                                             start=i == 0, stop=i == 2)
                        last.then_inc(hidden1, 1)
                        if not start:
                            output(k - 1, (e - 1) % E, f)
                    if start:
                        pe.wait_ge(w_low, 1)
                    else:
                        pe.wait_ge(spread_out, k)
                        pe.sem_inc(passed, 1)
                    for half in range(2):
                        last = pe.matmul(ps_t[:, 1, 0:TQ], sel1_sb[:, e, :], w_halves[:, half, tokens(c)],
                                         start=half == 0, stop=half == 1)
                    last.then_inc(spread1, 1)
                    if e == 0:
                        if not first:
                            pe.wait_ge(acc_set, c)
                            pe.sem_inc(passed, 1)
                        pe.matmul(ps_t[:, 2, 0:TQ], b2_sb[:, 1, :], wT[:, tokens(c)], start=True, stop=True).then_inc(b2_sum, 1)

            chunks(pe, body)
            for f in range(FK):
                output(E * NQ - 1, E - 1, f)
            pe.wait_ge(mixed1, NQ)
            for i in range(TT):
                last = pe.transpose(four_tiles(i), resid[:, P * i:P * (i + 1)], id_sb[:, :])
                if i % 4 == 3 or i == TT - 1:
                    last.then_inc(out_raw, 1)

        def mixture1_scalar(act):
            act.wait_ge(ln_done, NQ * 4)
            for c in range(NQ):
                act.activation(x_halves[:, 0, norm_cols(c)], normed[:, norm_cols(c)], ACT.Copy).then_inc(x_high, 1)
            route_scalar(act, 1)
            act.wait_ge(wT_done, 2 * NQ)
            act.activation(w_halves[:, 0, :], wT[:, :], ACT.Copy).then_inc(w_high, 1)

            def body(c, first=False):
                for e in range(E):
                    k = E * c + e
                    for f in range(FK):
                        act.wait_ge(hidden1, FK * k + f + 1)
                        if not isinstance(k, int) or k >= 1:
                            act.wait_ge(hid_low, FK * (k - 1) + f + 1)
                        act.activation(whole[:, f, :], hidden_bank(f), ACT.Relu, bias=b11_sb[:, e, f:f + 1])
                        if not isinstance(k, int) or k >= 2:
                            act.wait_ge(y_done, k - 1)
                        act.activation(halves[:, e % 2, 0, f, :], hidden_bank(f), ACT.Relu, bias=b11_sb[:, e, f:f + 1]).then_inc(hid_high, 1)
                    act.wait_ge(spread1, k + 1)
                    if not isinstance(k, int) or k >= 2:
                        act.wait_ge(y_mul, k - 1)
                    act.activation(work[:, e % 2, :], ps_t[:, 1, 0:TQ], ACT.Copy).then_inc(spread_out, 1)

            chunks(act, body)

        def mixture1_vector(dve):
            for c in range(NQ):
                dve.wait_ge(x_high, c + 1)
                dve.tensor_tensor(x_halves[:, 1, norm_cols(c)], normed[:, norm_cols(c)], x_halves[:, 0, norm_cols(c)],
                                  ALU.subtract).then_inc(x_low, 1)
            route_vector(dve, 1)
            dve.wait_ge(w_high, 1)
            dve.tensor_tensor(w_halves[:, 1, :], wT[:, :], w_halves[:, 0, :], ALU.subtract).then_inc(w_low, 1)
            prod, total = work[:, 2, :], work[:, 3, :]

            def weigh(k, e):
                dve.wait_ge(y_done, k + 1)
                dve.wait_ge(spread_out, k + 1)
                if not isinstance(k, int) or k >= 1:
                    dve.wait_ge(y_add, k)
                dve.tensor_tensor(prod, y1_bank(e), work[:, e % 2, :], ALU.mult).then_inc(y_mul, 1)
                dve.wait_ge(y_mul, k + 1)
                dve.tensor_tensor(total, total, prod, ALU.add).then_inc(y_add, 1)

            def finish(c):
                dve.wait_ge(y_add, E * (c + 1))
                r = resid[:, tokens(c)]
                dve.scalar_tensor_tensor(out=r, in0=total, scalar=gates[:, 3:4], in1=r, op0=ALU.mult, op1=ALU.add).then_inc(mixed1, 1)

            def body(c, first=False):
                for e in range(E):
                    k = E * c + e
                    for f in range(FK):
                        dve.wait_ge(hid_high, FK * k + f + 1)
                        if not isinstance(k, int) or k >= 2:
                            dve.wait_ge(y_done, k - 1)
                        dve.tensor_tensor(halves[:, e % 2, 1, f, :], whole[:, f, :], halves[:, e % 2, 0, f, :],
                                          ALU.subtract).then_inc(hid_low, 1)
                    if not (first and e == 0):
                        weigh(k - 1, (e - 1) % E)
                    if e == 0:
                        if not first:
                            finish(c - 1)
                            dve.wait_ge(mixed1, c)
                        dve.wait_ge(b2_sum, c + 1)
                        dve.tensor_copy(total, ps_t[:, 2, 0:TQ]).then_inc(acc_set, 1)
                        dve.wait_ge(acc_set, c + 1)

            chunks(dve, body)
            weigh(E * NQ - 1, E - 1)
            finish(NQ - 1)
            for c in range(NQ):
                n = min(4, TT - 4 * c)
                dve.wait_ge(out_raw, c + 1)
                bank = ps_s[:, c, :] if c < TH else ps_t[:, 0, :]
                dve.tensor_copy(xin[:, 4 * c:4 * c + n, :].rearrange("p i d -> p (i d)"), bank[:, 0:P * n]).then_inc(out_sb, 1)

        block = stack.enter_context(nc.Block())

        def batches(eng, batch):
            rounds(eng, batch, B)

        @block.sync
        def _(sp):
            def load_keys(b, w):
                sp.dma_start(ring[w][0:KP, :].rearrange("p (c d) -> p c d", d=D),
                             ctx_v[bass.ds(b, 1), :, :, :].rearrange("a p c d -> p (a c) d")).then_inc(keys_in[w], 16)

            def stack_keys(b, u):
                sp.wait_ge(kt_done, TH * (b + 1))
                if not isinstance(b, int) or b > 1:
                    if not isinstance(b, int):
                        sp.sem_inc(passed, 1)
                    sp.wait_ge(scored, TH * TILES * (b - 1))
                for term, half in enumerate((0, 0, 1)):
                    for g in range(NG):
                        sp.dma_start(kst[GD * term:GD * (term + 1), u, KTE * TH * g:KTE * TH * (g + 1)],
                                     kT16[GD * g:GD * (g + 1), half, :]).then_inc(kst_in, 16)

            sp.dma_start(id_sb[:, :], ident).then_inc(ident_in, 16)
            sp.dma_start(xin, x.rearrange("b s d -> (b s) d").rearrange("(i p) d -> p i d", p=P)).then_inc(x_in, 16)
            load_keys(0, 0)
            for dst, src in early:
                sp.dma_start(dst, src).then_inc(early_in, 16)
            for dst, src in consts:
                sp.dma_start(dst, src).then_inc(consts_in, 16)
            sp.dma_start(bias_sb[:, :, :], bias_v).then_inc(bias_in, 16)
            load_keys(1, 1)
            load_keys(2, 2)
            stack_keys(0, 0)
            for term, half, ready in ((0, h16, q_high), (2, h16, q_high), (1, l16, q_low)):
                sp.wait_ge(ready, 1)
                for g in range(NG):
                    sp.dma_start(qst[GD * term:GD * (term + 1), g, :], half[GD * g:GD * (g + 1), :]).then_inc(qst_in, 16)
            load_keys(3, 3)

            stack_keys(1, 1)

            def batch(b, w):
                stack_keys(b + 1, (w + 1) % 2)
                sp.wait_ge(values_used, b)
                sp.sem_inc(passed, 1)
                load_keys(b + RING - 1, (w - 1) % RING)

            with sp.Fori(0, B // RING - 1) as i:
                for d in range(1, RING + 1):
                    batch(RING * i + d, d % RING)
            stack_keys(B - 2, 0)
            stack_keys(B - 1, 1)
            second_attention_sync(sp)

        @block.gpsimd
        def _(pool):
            def low(b, w, j):
                pool.wait_ge(k_high, TH * b + j + 1)
                s = third(j)
                pool.tensor_tensor(k16[0:KP, 1, s], ring[w][0:KP, s], k16[0:KP, 0, s], ALU.subtract).then_inc(k_low, 1)

            def queries(b, u, first=False):
                if not first:
                    pool.wait_ge(scored, TH * TILES * (b - 1))
                for g in range(NG):
                    dst = qbd[0:ST, u, GR * g:GR * (g + 1)].rearrange("p (h q) -> p h q", h=GH)
                    q = qst[0:ST, g, bass.ds(S * b, S)].unsqueeze(1).broadcast_to([ST, GH, S])
                    m = diag4h_sb[0:ST, :].unsqueeze(2).broadcast_to([ST, GH, S])
                    done = pool.tensor_tensor(dst, q, m, ALU.mult)
                done.then_inc(q_ready, 1)

            def row_sums(b, u, first=False):
                pool.wait_ge(probs, TILES * (b + 1))
                if not first:
                    pool.wait_ge(attended, b)
                pool.sem_inc(passed, 1)
                pool.tensor_copy(rs16[:, 0, :], rowsum[:, u, :]).then_inc(rs_part, 1)
                pool.wait_ge(rs_part, 2 * b + 1)
                pool.tensor_tensor(rs16[:, 1, :], rowsum[:, u, :], rs16[:, 0, :], ALU.subtract).then_inc(rs_part, 1)
                pool.wait_ge(rs_part, 2 * b + 2)
                for half in range(2):
                    r = rs16[:, half, :].unsqueeze(2).broadcast_to([P, TILES, S])
                    done = pool.tensor_tensor(rsel[:, half, :, :], rowq_sb[:, :, :], r, ALU.mult)
                done.then_inc(rsel_done, 1)

            for j in range(TH):
                low(0, 0, j)
            pool.wait_ge(consts_in, CONSTS)
            pool.wait_ge(qst_in, STACKED)
            queries(0, 0, first=True)
            for j in range(TH):
                low(1, 1, j)

            def batch(b, w, k, left, first=False):
                u = w % 2
                if left > 0:
                    queries(b + 1, 1 - u, first=first)
                if left > 1:
                    for j in range(TH):
                        low(b + 2, (w + 2) % RING, j)
                row_sums(b, u, first=first)

            batches(pool, batch)
            split_weights(pool)
            second_attention_pool(pool)

        @block.scalar
        def _(act):
            def keys_out(b, j):
                act.wait_ge(kt_raw, TH * b + j + 1)
                if not isinstance(b, int) or b > 0:
                    act.wait_ge(kst_in, STACKED * b)
                act.activation(kT16[:, :, KTE * j:KTE * (j + 1)], ps_kt[:, :, 0:KTE], ACT.Copy).then_inc(kt_done, 1)

            for j in range(TH):
                keys_out(0, j)
            norm_scalar(act, 0)
            act.wait_ge(ln_done, NQ)
            act.activation(h16, normed[:, :], ACT.Copy).then_inc(q_high, 1)
            act.wait_ge(consts_in, CONSTS)
            act.activation(gates[:, :], gates_in[:, :], ACT.Tanh).then_inc(gates_done, 1)

            def evacuate(n, u, t, q):
                act.wait_ge(t_raw, TH * n + q + 1)
                act.activation(transposed(u, t, q),
                               ps_t[0:KP, q, :].rearrange("p (c r) -> p c r", r=P), ACT.Copy).then_inc(t_act, 1)

            def exponent(n, s, t, u):
                act.wait_ge(negmaxed, n + 1)
                act.activation(sc[:, s, :], sc[:, s, :], ACT.Exp, bias=negmax[:, s:s + 1],
                               accum_out=rowsum[:, u, t:t + 1]).then_inc(probs, 1)

            def batch(b, w, k, left, first=False):
                u = w % 2
                for t in range(TILES):
                    n = TILES * b + t
                    if t == TILES - 1 and left > 0 and not first:
                        act.wait_ge(rsel_done, b)
                    before = (n - 1, u if t > 0 else 1 - u, (t - 1) % TILES)
                    if not (first and t == 0):
                        evacuate(*before, 0)
                    exponent(n, (u + t) % 2, t, u)
                    if not (first and t == 0):
                        evacuate(*before, 1)
                    if t == 0 and left > 0:
                        keys_out(b + 1, 2)
                    if t in (4, 6) and left > 1:
                        keys_out(b + 2, (t - 4) // 2)

            for j in range(2):
                keys_out(1, j)
            batches(act, batch)
            evacuate(TILES * B - 1, 1, TILES - 1, 0)
            evacuate(TILES * B - 1, 1, TILES - 1, 1)
            norm_scalar(act, 1)
            mixture0_scalar(act)
            norm_scalar(act, 2)
            second_attention_scalar(act)
            norm_scalar(act, 3)
            mixture1_scalar(act)

        @block.vector
        def _(dve):
            dve.memset(eps_sb[:, :], EPS / D ** 2).then_inc(eps_set, 1)
            dve.memset(k16[96:P, :, :], 0.0).then_inc(k_zero, 1)
            for c in range(NQ):
                n = min(4, TT - 4 * c)
                dve.wait_ge(xT_raw, c + 1)
                src = (ps_s[:, c, :] if c < TH else ps_t[:, 0, :])[:, 0:P * n]
                dve.tensor_copy(resid[:, 4 * P * c:4 * P * c + P * n], src).then_inc(xT_done, 1)
            def high(b, w, k, j):
                dve.wait_ge(keys_in[w], 16 * (k + 1))
                if not isinstance(b, int) or b > 0:
                    dve.wait_ge(kt_raw, TH * (b - 1) + j + 1)
                dve.tensor_copy(k16[0:KP, 0, third(j)], ring[w][0:KP, third(j)]).then_inc(k_high, 1)

            dve.wait_ge(k_zero, 1)
            for j in range(TH):
                high(0, 0, 0, j)
            norm_vector(dve, 0)
            dve.wait_ge(ln_done, NQ)
            dve.wait_ge(q_high, 1)
            dve.tensor_tensor(l16, normed[:, :], h16, ALU.subtract).then_inc(q_low, 1)
            dve.wait_ge(b1_raw, 1)
            dve.tensor_copy(b1T[:, :], ps_o[:, 0:B1R]).then_inc(b1_done, 1)

            def bias_max(n, s, u, t, start=False):
                for j in range(TH):
                    if j == TH - 1 and not start:
                        evacuate(n - 2, u if t > 1 else 1 - u, (t - 2) % TILES)
                    dve.wait_ge(scored, TH * n + j + 1)
                    if not isinstance(n, int) or n >= 2:
                        dve.wait_ge(t_raw, TH * (n - 2) + j + 1)
                    dve.sem_inc(passed, 1)
                    dve.tensor_tensor_reduce(
                        out=sc[:, s, KT * j:KT * (j + 1)], in0=ps_s[:, j, 0:KT], in1=bias_sb[:, t, KT * j:KT * (j + 1)],
                        scale=SCALE0, scalar=-3.0e38, op0=ALU.add, op1=ALU.max,
                        accum_out=mx[:, s, j:j + 1]).then_inc(biased, 1)
                dve.wait_ge(biased, TH * (n + 1))
                dve.tensor_reduce(negmax[:, s:s + 1], mx[:, s, :], axis=AX.X, op=ALU.max,
                                  negate=True).then_inc(negmaxed, 1)

            def evacuate(n, u, t):
                dve.wait_ge(t_raw, TH * (n + 1))
                dve.tensor_copy(transposed(u, t, 2),
                                ps_t[0:KP, 2, :].rearrange("p (c r) -> p c r", r=P)).then_inc(t_dve, 1)

            def combine(b):
                dve.wait_ge(attended, b + 1)
                m = diag4_sb[:, :].unsqueeze(2).broadcast_to([P, GH, S])
                dve.tensor_tensor(o_mask[:, :, :], pv_acc.rearrange("p (h q) -> p h q", h=GH), m, ALU.mult).then_inc(comb_step, 1)
                dve.reciprocal(r_inv[:, :], r_acc).then_inc(comb_step, 1)
                dve.wait_ge(comb_step, 3 * b + 1)
                dve.tensor_reduce(o_sum[:, :], o_mask[:, :, :].rearrange("p h q -> p q h"), axis=AX.X, op=ALU.add
                                  ).then_inc(comb_step, 1)
                dve.wait_ge(comb_step, 3 * b + 3)
                dve.tensor_tensor(comb[:, :], o_sum[:, :], r_inv[:, :], ALU.mult).then_inc(combined, 1)

            def update(b):
                dve.wait_ge(projected, b + 1)
                r = resid[:, bass.ds(S * b, S)]
                dve.scalar_tensor_tensor(out=r, in0=ps_m[:, 0:S], scalar=gates[:, 0:1], in1=r,
                                         op0=ALU.mult, op1=ALU.add).then_inc(updated, 1)

            for j in range(TH):
                high(1, 1, 0, j)
            dve.wait_ge(bias_in, 16)
            dve.wait_ge(gates_done, 1)

            def batch(b, w, k, left, first=False):
                u = w % 2
                for t in range(TILES):
                    n = TILES * b + t
                    bias_max(n, (u + t) % 2, u, t, start=first and t < 2)
                    if not first and t == 4:
                        combine(b - 1)
                    if not first and t == 5:
                        update(b - 1)
                    if left > 1 and t == 1:
                        for j in range(TH):
                            high(*ahead(b, w, k, 2), j)

            batches(dve, batch)
            evacuate(TILES * B - 2, 1, TILES - 2)
            evacuate(TILES * B - 1, 1, TILES - 1)
            combine(B - 1)
            update(B - 1)
            norm_vector(dve, 1)
            mixture0_vector(dve)
            norm_vector(dve, 2)
            second_attention_vector(dve)
            norm_vector(dve, 3)
            mixture1_vector(dve)

        @block.tensor
        def _(pe):
            pe.wait_ge(ident_in, 16)
            pe.wait_ge(x_in, 16)
            for i in range(TT):
                c = i // 4
                dst = (ps_s[:, c, :] if c < TH else ps_t[:, 0, :])[:, P * (i % 4):P * (i % 4 + 1)]
                last = pe.transpose(dst, xin[:, i, :], id_sb[:, :])
                if i % 4 == 3 or i == TT - 1:
                    last.then_inc(xT_raw, 1)
            pe.wait_ge(early_in, 16 * len(early))
            centre_tensor(pe, 0)
            def keys(b, j):
                pe.wait_ge(k_low, TH * b + j + 1)
                if isinstance(b, int) and b == 0:
                    if j > 0:
                        pe.wait_ge(kt_done, j)
                else:
                    pe.wait_ge(kt_done, TH * b + j)
                if j == 1 and (not isinstance(b, int) or b > 2):
                    pe.wait_ge(updated, b - 2)
                for half in range(2):
                    for c in range(CT):
                        cc = CT * j + c
                        last = pe.transpose(ps_kt[:, half, KE * c:KE * (c + 1)],
                                            k16[0:KE, half, D * cc:D * (cc + 1)], id16_sb[0:KE, 0:KE])
                last.then_inc(kt_raw, 1)

            for j in range(TH):
                keys(0, j)
            pe.wait_ge(kt_done, TH)
            norm_tensor(pe, 0)
            pe.wait_ge(consts_in, CONSTS)
            pe.wait_ge(ln_done, NQ)
            pe.transpose(ps_o[:, 0:B1R], b1_rows[:, :], id_sb[0:B1R, 0:B1R]).then_inc(b1_raw, 1)

            def scores(b, u, n, t, j):
                if t == 0 and j == 0:
                    pe.wait_ge(q_ready, b + 1)
                    pe.wait_ge(kst_in, STACKED * (b + 1))
                if not isinstance(n, int) or n > 0:
                    pe.wait_ge(biased, TH * (n - 1) + j + 1)
                for g, r, m in pieces(t):
                    at = r - P * t
                    stack_ = kst[0:ST, u, KTE * (TH * g + j):KTE * (TH * g + j + 1)].rearrange("p (c k) -> p c k", k=KE)
                    last = pe.matmul(ps_s[at:at + m, j, 0:KT], qbd[0:ST, u, r:r + m], stack_[:, :, 0:KP],
                                     start=True, stop=True)
                last.then_inc(scored, 1)

            def transposes(n, s, q):
                if q == 0:
                    pe.wait_ge(probs, n + 1)
                if not isinstance(n, int) or n > 0:
                    if q < 2:
                        pe.wait_ge(t_act, 2 * (n - 1) + q + 1)
                    else:
                        pe.wait_ge(t_dve, n)
                for c in range(CT):
                    cc = CT * q + c
                    last = pe.transpose(ps_t[0:KP, q, P * c:P * (c + 1)], sc[:, s, KP * cc:KP * (cc + 1)], id_sb[:, :])
                last.then_inc(t_raw, 1)

            def attend(b, w, q):
                if q == 0:
                    pe.wait_ge(t_act, 2 * TILES * (b + 1))
                if q == TH - 1:
                    pe.wait_ge(t_dve, TILES * (b + 1))
                for c in range(CT * q, CT * (q + 1)):
                    for g in range(NG):
                        values = ring[w][0:KP, D * c + GD * g:D * c + GD * (g + 1)]
                        done = min(max(XT * P - GR * g, 0), GR) if w % 2 == 1 else 0
                        if done > 0:
                            at = XT * P * c + GR * g
                            last = pe.matmul(ps_o[GD * g:GD * (g + 1), 0:done], values, ptX[0:KP, at:at + done],
                                             start=c == 0, stop=c == KC - 1 and done == GR)
                        if done < GR:
                            at = ROWS * c + GR * g
                            last = pe.matmul(ps_o[GD * g:GD * (g + 1), done:GR], values, ptT[0:KP, at + done:at + GR],
                                             start=c == 0 and done == 0, stop=c == KC - 1)
                if q == TH - 1:
                    last.then_inc(values_used, 1)

            def spread_sums(b):
                pe.wait_ge(rsel_done, b + 1)
                for t in range(TILES):
                    for half in range(2):
                        last = pe.matmul(r_acc, rowhead_sb[:, t, :], rsel[:, half, t, :],
                                         start=t == 0 and half == 0, stop=t == TILES - 1 and half == 1)
                last.then_inc(attended, 1)

            def project(b):
                pe.wait_ge(combined, b + 1)
                if not isinstance(b, int) or b < B - 1:
                    pe.wait_ge(kt_done, TH * (b + 3) + 1 if not isinstance(b, int) or b < B - 3 else TH * B)
                pe.matmul(ps_m[:, 0:S], wout_sb[:, :], comb[:, :], start=True, stop=True).then_inc(projected, 1)

            for j in range(TH):
                scores(0, 0, 0, 0, j)
            for j in range(2):
                keys(1, j)

            def batch(b, w, k, left, first=False):
                u = w % 2
                for t in range(TILES):
                    n = TILES * b + t
                    for j in range(TH):
                        if not first and t == 5 and j == 1:
                            project(b - 1)
                        if t < TILES - 1:
                            scores(b, u, n + 1, t + 1, j)
                        elif left > 0:
                            scores(b + 1, 1 - u, n + 1, 0, j)
                        if not first and t == 1 + XT and j == 2:
                            attend(b - 1, (w - 1) % RING, j)
                        if not (first and t == 0):
                            transposes(n - 1, (u + t + 1) % 2, j)
                    if not first and t in (1, 2):
                        attend(b - 1, (w - 1) % RING, t - 1)
                    if not first and t == 3:
                        spread_sums(b - 1)
                    if left > 0 and t == 0:
                        keys(b + 1, 2)
                    if left > 1 and t in (4, 6):
                        keys(b + 2, (t - 4) // 2)

            batches(pe, batch)
            for j in range(TH):
                transposes(TILES * B - 1, (1 + TILES - 1) % 2, j)
            for j in range(TH):
                attend(B - 1, RING - 1, j)
            spread_sums(B - 1)
            project(B - 1)
            norm_tensor(pe, 1)
            mixture0_tensor(pe)
            norm_tensor(pe, 2)
            second_attention_tensor(pe)
            norm_tensor(pe, 3)
            mixture1_tensor(pe)


_INS = ["x", "ctx_1024", "fside_1x16xSxS2_0", "g_xattn", "g_ffn", "L0_xattn_w_out", "L0_ffn_router_w",
        "L0_ffn_router_b", "L0_ffn_W1", "L0_ffn_b1", "L0_ffn_W2", "L0_ffn_b2", "L1_xattn_scale_factor",
        "L1_ffn_W_router", "L1_ffn_b_router", "L1_ffn_W1", "L1_ffn_b1", "L1_ffn_W2", "L1_ffn_b2"]


def _constants():
    import numpy as np

    row = np.arange(ROWS).reshape(TILES, P).T
    part = np.arange(P)
    one = {
        "ident": np.eye(P, dtype=np.float32),
        "ident16": np.eye(P, dtype=np.float16),
        "diag4": (part[:, None] % GD // HD == np.arange(GH)).astype(np.float32),
        "diag4h": (part[:ST, None] % GD // HD == np.arange(GH)).astype(np.float16),
        "row_q": (row[:, :, None] % S == np.arange(S)).astype(np.float16),
        "row_head": (row[:, :, None] // S == part // HD).astype(np.float16),
        "sel0": (np.arange(E)[:, None, None] == 2 * np.arange(E // 2)[:, None] + part // F0).astype(np.float32),
        "sel1": np.broadcast_to(np.eye(E, dtype=np.float16)[:, :, None], (E, E, P)).copy(),
        "mean_w": np.full((P, P), 1.0 / D, np.float32),
        "centre_w": (np.eye(P) - 1.0 / D).astype(np.float32),
        "rank": np.broadcast_to(np.arange(E, 0, -1, dtype=np.float32), (P, E)).copy(),
    }
    return one


def kernel(**inputs):
    import numpy as _np
    import concourse.bacc as _bacc
    from concourse import mybir as _mybir
    from concourse.bass_utils import run_bass_kernel_spmd as _run

    nc = _bacc.Bacc("TRN2", target_bir_lowering=False, num_devices=1)
    arrays, args = {}, []
    for name in _INS:
        a = _np.ascontiguousarray(inputs[name])
        if a.ndim == 0:
            a = a.reshape(1)
        arrays[f"in_{name}_dram"] = a
        args.append(nc.dram_tensor(f"in_{name}_dram", a.shape, _mybir.dt.from_np(a.dtype), kind="ExternalInput").ap())
    for name, a in _constants().items():
        arrays[f"const_{name}_dram"] = a
        args.append(nc.dram_tensor(f"const_{name}_dram", a.shape, _mybir.dt.from_np(a.dtype), kind="ExternalInput").ap())
    args.append(nc.dram_tensor("out_dram", (B, S, D), _mybir.dt.float32, kind="ExternalOutput").ap())
    flamingo(nc, *args)
    r = _run(nc, [arrays], core_ids=[0])
    return r.results[0]["out_dram"]
```
